# Optimizing a Trainium2 kernel written in Bass

```python
import numpy as np
import jax
import jax.numpy as jnp

def _softmax(x, axis=-1):
    return jax.nn.softmax(x, axis=axis)

def _gelu(x):
    return jax.nn.gelu(x, approximate=True)

def _silu(x):
    return jax.nn.silu(x)

def _sigmoid(x):
    return jax.nn.sigmoid(x)

def _layernorm(x, axis=-1, eps=1e-05):
    m = jnp.mean(x, axis=axis, keepdims=True)
    v = jnp.var(x, axis=axis, keepdims=True)
    return (x - m) / jnp.sqrt(v + eps)

def _scatter_add(tgt, idx, src, axis=0):
    return tgt.at[idx].add(src)

def _segment_sum(src, seg, n):
    return jax.ops.segment_sum(src, seg, n)
kernel_name = 'mk_gnn_resnorm_d1_gnn_r32_7b1ed2'

def setup_inputs(seed: int=0):
    np.random.seed(seed)
    _w = jnp.asarray

    def _rec_inputs():
        import jax
        import jax.numpy as jnp
        _gk = jax.random.key(seed)
        x = -0.0005121 + 1.001 * jax.random.normal(jax.random.fold_in(_gk, 1), (50000, 160), jnp.float32)
        src = jax.random.randint(jax.random.fold_in(_gk, 2), (50000,), 0, 50000, jnp.int32)
        dst = jax.random.randint(jax.random.fold_in(_gk, 3), (50000,), 0, 50000, jnp.int32)
        _o = jnp.argsort(dst, stable=True)
        src = src[_o]
        dst = dst[_o]
        edge_attr_16 = -0.000191324 + 0.999809 * jax.random.normal(jax.random.fold_in(_gk, 12), (50000, 16), jnp.float32)
        edge_attr_4 = 0.000126197 + 0.999763 * jax.random.normal(jax.random.fold_in(_gk, 13), (50000, 4), jnp.float32)
        node_vec1 = jax.random.uniform(jax.random.fold_in(_gk, 14), (50000, 1), jnp.float32, 0.0, 1)
        return (x, src, dst, edge_attr_16, edge_attr_4, node_vec1)
    x, src, dst, edge_attr_16, edge_attr_4, node_vec1 = _rec_inputs()

    def _L0_gnn_setup():
        import jax, jax.numpy as jnp
        import numpy as np
        N = 625
        E = 10000
        MUL0 = 64
        MUL1 = 32
        FC_IN = 16
        FC_H = 64
        WNUM = 192
        key = jax.random.key(seed)
        ks = jax.random.split(key, 16)
        return {'x': jax.random.normal(ks[0], (N, MUL0 + 3 * MUL1), jnp.float32), 'node_attr': jnp.ones((N, 1), jnp.float32), 'edge_scalars': jax.random.normal(ks[1], (E, FC_IN), jnp.float32), 'edge_attr_sh': jax.random.normal(ks[2], (E, 4), jnp.float32), 'edge_src': jax.random.randint(ks[3], (E,), 0, N), 'edge_dst': jax.random.randint(ks[4], (E,), 0, N), 'Wfc1': jax.random.normal(ks[5], (FC_IN, FC_H), jnp.float32), 'Wfc2': jax.random.normal(ks[6], (FC_H, WNUM), jnp.float32), 'Wsc0': jax.random.normal(ks[7], (MUL0, MUL0), jnp.float32), 'Wsc1': jax.random.normal(ks[8], (MUL1, MUL1), jnp.float32), 'Wl1_0': jax.random.normal(ks[9], (MUL0, MUL0), jnp.float32), 'Wl1_1': jax.random.normal(ks[10], (MUL1, MUL1), jnp.float32), 'Wl2_s': jax.random.normal(ks[11], (MUL0 + MUL1, MUL0), jnp.float32), 'Wl2_v': jax.random.normal(ks[12], (MUL0 + MUL1, MUL1), jnp.float32), 'Wa': 0.1 * jax.random.normal(ks[13], (MUL0 + MUL1, 1), jnp.float32)}
    _L0_gnn_all = _L0_gnn_setup()
    _L0_gnn_in = {k: v for k, v in _L0_gnn_all.items() if k in ('Wfc1', 'Wfc2', 'Wsc0', 'Wsc1', 'Wl1_0', 'Wl1_1', 'Wl2_s', 'Wl2_v', 'Wa')}
    del _L0_gnn_all
    return {'x': x, 'src': src, 'dst': dst, 'edge_attr_16': edge_attr_16, 'edge_attr_4': edge_attr_4, 'node_vec1': node_vec1, 'L0_gnn_Wfc1': _L0_gnn_in['Wfc1'], 'L0_gnn_Wfc2': _L0_gnn_in['Wfc2'], 'L0_gnn_Wsc0': _L0_gnn_in['Wsc0'], 'L0_gnn_Wsc1': _L0_gnn_in['Wsc1'], 'L0_gnn_Wl1_0': _L0_gnn_in['Wl1_0'], 'L0_gnn_Wl1_1': _L0_gnn_in['Wl1_1'], 'L0_gnn_Wl2_s': _L0_gnn_in['Wl2_s'], 'L0_gnn_Wl2_v': _L0_gnn_in['Wl2_v'], 'L0_gnn_Wa': _L0_gnn_in['Wa']}

def reference(x, src, dst, edge_attr_16, edge_attr_4, node_vec1, L0_gnn_Wfc1, L0_gnn_Wfc2, L0_gnn_Wsc0, L0_gnn_Wsc1, L0_gnn_Wl1_0, L0_gnn_Wl1_1, L0_gnn_Wl2_s, L0_gnn_Wl2_v, L0_gnn_Wa):
    import jax
    import jax.numpy as jnp

    def _L0_gnn_ref(x, node_attr, edge_scalars, edge_attr_sh, edge_src, edge_dst, Wfc1, Wfc2, Wsc0, Wsc1, Wl1_0, Wl1_1, Wl2_s, Wl2_v, Wa):
        import jax, jax.numpy as jnp
        import numpy as np
        N = 625
        E = 10000
        MUL0 = 64
        MUL1 = 32
        FC_IN = 16
        FC_H = 64
        WNUM = 192
        n = x.shape[0]
        x0 = x[:, :MUL0]
        x1 = x[:, MUL0:].reshape(n, MUL1, 3)
        a = node_attr
        h = jax.nn.silu(edge_scalars @ (Wfc1 / jnp.sqrt(jnp.float32(FC_IN))))
        w = h @ (Wfc2 / jnp.sqrt(jnp.float32(FC_H)))
        w0 = w[:, :64]
        w1 = w[:, 64:128]
        w2 = w[:, 128:160]
        w3 = w[:, 160:192]
        inv8 = 1.0 / jnp.sqrt(jnp.float32(MUL0))
        inv32 = 1.0 / jnp.sqrt(jnp.float32(MUL1))
        sc = jnp.concatenate([x0 @ Wsc0 * a * inv8, (jnp.einsum('num,uv->nvm', x1, Wsc1) * a[..., None] * inv32).reshape(n, 3 * MUL1)], axis=1)
        f0 = x0 @ Wl1_0 * a * inv8
        f1 = jnp.einsum('num,uv->nvm', x1, Wl1_1) * a[..., None] * inv32
        e0 = f0[edge_src]
        e1 = f1[edge_src]
        sh0 = edge_attr_sh[:, :1]
        sh1 = edge_attr_sh[:, 1:4]
        mid0 = w0 * e0 * sh0
        mid1 = w3 * jnp.einsum('eum,em->eu', e1, sh1) / jnp.sqrt(3.0)
        mid2 = w1[:, :, None] * e0[:, :, None] * sh1[:, None, :]
        mid3 = w2[:, :, None] * e1 * sh0[:, :, None]
        cnt = jnp.clip(jax.ops.segment_sum(jnp.ones(edge_dst.shape, x.dtype), edge_dst, num_segments=n), 1.0)

        def smean(v):
            s = jax.ops.segment_sum(v, edge_dst, num_segments=n)
            return s / cnt.reshape((n,) + (1,) * (v.ndim - 1))
        n0, n1 = (smean(mid0), smean(mid1))
        n2, n3 = (smean(mid2), smean(mid3))
        scal = jnp.concatenate([n0, n1], axis=1)
        vec = jnp.concatenate([n2, n3], axis=1)
        inv96 = 1.0 / jnp.sqrt(jnp.float32(MUL0 + MUL1))
        alpha = scal @ Wa * a * inv96
        out_s = scal @ Wl2_s * a * inv96
        out_v = jnp.einsum('num,uv->nvm', vec, Wl2_v) * a[..., None] * inv96
        conv = jnp.concatenate([out_s, out_v.reshape(n, 3 * MUL1)], axis=1)
        return sc + alpha * conv
    x = _layernorm(x + _L0_gnn_ref(x, node_vec1, edge_attr_16, edge_attr_4, src, dst, L0_gnn_Wfc1, L0_gnn_Wfc2, L0_gnn_Wsc0, L0_gnn_Wsc1, L0_gnn_Wl1_0, L0_gnn_Wl1_1, L0_gnn_Wl2_s, L0_gnn_Wl2_v, L0_gnn_Wa), axis=-1)
    return x

_drawn_inputs = setup_inputs


def setup_inputs(seed=0):
    import zlib

    import numpy as np

    out = dict(_drawn_inputs(seed))
    spreads = {}
    factors = {'edge_attr_16': 8.0,
     'edge_attr_4': 8.0,
     'L0_gnn_Wfc1': 8.0,
     'L0_gnn_Wfc2': 8.0,
     'L0_gnn_Wl1_0': 8.0,
     'L0_gnn_Wl1_1': 8.0,
     'L0_gnn_Wl2_s': 8.0,
     'L0_gnn_Wl2_v': 8.0,
     'L0_gnn_Wa': 8.0}
    for name, (base, spread) in spreads.items():
        noise = np.random.default_rng([zlib.crc32(name.encode()), seed]).standard_normal(out[name].shape)
        drawn = base * np.exp(spread * noise) if base else spread * noise
        out[name] = jnp.asarray(drawn.astype(out[name].dtype))
    for name, factor in factors.items():
        out[name] = (out[name] * factor).astype(out[name].dtype)
    return out
```

```python
from contextlib import ExitStack

import concourse.bass as bass
from concourse import mybir

P = 128
F32 = mybir.dt.float32
I32 = mybir.dt.int32
ALU = mybir.AluOpType
ACT = mybir.ActivationFunctionType
AX_X = mybir.AxisListType.X

MUL0, MUL1 = 64, 32
VEC = 3 * MUL1
D = MUL0 + VEC
FC_IN, FC_H = 16, 64
HID = MUL0 + MUL1
BLOCK = 8
PAIRS = BLOCK // 2
GROUP = 4
RING = 4
EPS = 1e-5

XW = 1 + D
QX = XW
GW = XW + MUL1
GATE, CNT = 0, 1 + D
AW = 2 + D
Y_B, Y_X, Y_C = 0, MUL1, MUL1 + 1 + D
YW = Y_C + 1 + MUL0

W_H = 0
W_W = W_H + PAIRS * P
W_E0 = W_W + 4 * P
W_E1 = W_E0 + P
W_Y0 = W_E1 + P
W_Y1 = W_Y0 + MUL1 + 1 + MUL0
W_S0 = W_Y1 + VEC + 1 + MUL0
W_S1 = W_S0 + MUL0
WC = W_S1 + VEC


def gnn_kernel(nc, table, src_t, dst_t, dst_rows, sh_t, ea_t, weights, out):
    NP = table.shape[0]
    T = src_t.shape[1]
    NB = T // BLOCK
    NQ = T // 2
    NG = NP // (P * GROUP)
    ROWS = NP + P
    DIRECT = 2
    LAG = 6
    assert NB > DIRECT + 1 and NG // RING > 1 and ROWS % P == 0

    inv8, inv32 = MUL0 ** -0.5, MUL1 ** -0.5
    inv96 = HID ** -0.5
    inv_fc = FC_H ** -0.5

    acc = [nc.dram_tensor(f"acc{s}", [ROWS, AW], F32, kind="Internal").ap() for s in range(2)]

    with ExitStack() as ctx:
        def sb(name, shape, dt=F32):
            return ctx.enter_context(nc.sbuf_tensor(name, shape, dt))

        def sem(name):
            return ctx.enter_context(nc.semaphore(name))

        ps = ctx.enter_context(nc.psum_tensor("ps", [P, 8, 512], F32))
        wt = sb("wt", [P, WC])
        wy = sb("wy", [P, W_S1 + VEC - W_Y0])
        ident = sb("ident", [P, P])
        later_mask = sb("later_mask", [P, P])
        srcs = sb("srcs", [P, T], I32)
        dsts_i = sb("dsts_i", [P, T], I32)
        dsts = sb("dsts", [P, T])
        spare = sb("spare", [P, T])
        shs = sb("shs", [P, T, 4])
        eas = sb("eas", [P, NB, P])
        zeros = sb("zeros", [P, 3, AW])

        src_now = sb("src_now", [P, BLOCK], I32)
        rows_now = sb("rows_now", [P, 2, 4 * P], I32)
        gat = sb("gat", [P, BLOCK, GW])
        sha = sb("sha", [P, PAIRS, 2, 4])
        qprod = sb("qprod", [P, 2, MUL1, 3])
        t_sb = sb("t_sb", [P, 2, 2, 2, P])
        h_sb = sb("h_sb", [P, 2, P])
        e_sb = sb("e_sb", [P, 2, 2, 2, P])
        mid = sb("mid", [P, 2, 2, 2, P])
        z = sb("z", [P, 2, 2, 1 + D])
        msg = sb("msg", [P, 2, 2, AW])
        same = sb("same", [P, 2, 2, P])
        junk = sb("junk", [P, 2, P])
        later = sb("later", [P, 2, 2])
        moved = sb("moved", [P, 2, 2])
        row_now = sb("row_now", [P, PAIRS, 2], I32)
        sums = sb("sums", [P, PAIRS, 2, AW])

        xin = sb("xin", [P, RING, GROUP, XW])
        acc_in = [sb(f"acc_in{s}", [P, RING, GROUP, AW]) for s in range(2)]
        agg = sb("agg", [P, RING, GROUP, AW])
        xt = sb("xt", [P, 2, 2, GROUP, P])
        pre = sb("pre", [P, 2, GROUP, D])
        res = sb("res", [P, 2, GROUP, D])
        fin = sb("fin", [P, 2, GROUP, D])
        cnt = sb("cnt", [P, 2, GROUP])
        rcnt = sb("rcnt", [P, 2, GROUP])
        ra = sb("ra", [P, 2, GROUP])
        rr = sb("rr", [P, 2, GROUP])
        coef = sb("coef", [P, 2, GROUP])
        stats = sb("stats", [P, 2, GROUP, 6])
        mv = sb("mv", [P, 2, GROUP, 2])
        eps = sb("eps", [P, 1])
        std = sb("std", [P, 2, GROUP])
        rstd = sb("rstd", [P, 2, GROUP])
        shift = sb("shift", [P, 2, GROUP])

        t_ps = ps[:, 0, :].rearrange("p (c s e) -> p c s e", c=2, s=2)
        h_ps = ps[:, 1, 0:P]
        e_ps = ps[:, 2, :].rearrange("p (c s e) -> p c s e", c=2, s=2)
        w_ps = ps[:, 3, :].rearrange("p (c s e) -> p c s e", c=2, s=2)
        y_ps = ps[:, 4:6, :]
        a_ps = ps[:, 6:8, :].rearrange("p b (s e) -> p b s e", s=2)
        xt_ps = ps[:, 0:4, :].rearrange("p (b c) (k e) -> p b c k e", b=2, k=GROUP)
        sc_ps = ps[:, 4:8, :].rearrange("p (b c) (k e) -> p b (c k) e", b=2, k=2)

        tables_in = sem("tables_in")
        weights_in = sem("weights_in")
        zeros_set = sem("zeros_set")
        acc_zero = sem("acc_zero")
        const_step = sem("const_step")
        const_ready = sem("const_ready")
        spare_base = sem("spare_base")
        dsts_ready = sem("dsts_ready")
        spare_ready = sem("spare_ready")
        wy_ready = sem("wy_ready")
        src_ready = sem("src_ready")
        gathered = [sem(f"gathered{n}") for n in range(BLOCK)]
        gather_go = sem("gather_go")
        scatter_go = sem("scatter_go")
        rows_in = [sem(f"rows_in{n}") for n in range(2)]
        sha_ready = sem("sha_ready")
        qprod_ready = sem("qprod_ready")
        q_ready = sem("q_ready")
        t_ready = sem("t_ready")
        t_out = sem("t_out")
        h_ready = sem("h_ready")
        h_out = sem("h_out")
        e_ready = sem("e_ready")
        e_out = sem("e_out")
        w_ready = sem("w_ready")
        mid_ready = sem("mid_ready")
        y_ready = sem("y_ready")
        zc_ready = sem("zc_ready")
        zb_ready = sem("zb_ready")
        msg_ready = sem("msg_ready")
        same_ready = sem("same_ready")
        later_ready = sem("later_ready")
        moved_ready = sem("moved_ready")
        row_ready = sem("row_ready")
        a_ready = sem("a_ready")
        sums_ready = sem("sums_ready")
        added = [sem(f"added{s}") for s in range(2)]

        x_in = [sem(f"x_in{b}") for b in range(RING)]
        acc_loaded = [sem(f"acc_loaded{b}") for b in range(RING)]
        agg_ready = sem("agg_ready")
        xt_ready = sem("xt_ready")
        xt_out = sem("xt_out")
        sc_ready = sem("sc_ready")
        cnt_ready = sem("cnt_ready")
        rcnt_ready = sem("rcnt_ready")
        ra_ready = sem("ra_ready")
        rr_ready = sem("rr_ready")
        coef_ready = sem("coef_ready")
        pre_ready = sem("pre_ready")
        res_ready = sem("res_ready")
        stats_ready = sem("stats_ready")
        mv_ready = sem("mv_ready")
        std_ready = sem("std_ready")
        rstd_ready = sem("rstd_ready")
        shift_ready = sem("shift_ready")
        fin_ready = sem("fin_ready")
        stored = [sem(f"stored{b}") for b in range(2)]

        block = ctx.enter_context(nc.Block())

        def edge_steps(engine, step):
            for i in range(DIRECT):
                for j in range(PAIRS):
                    step(i, j)
            with engine.Fori(DIRECT, NB) as i:
                for j in range(PAIRS):
                    step(i, j)
            for n in range(LAG):
                step(NB + n // PAIRS, n % PAIRS)

        def alive(i, j, behind):
            return not isinstance(i, int) or 0 <= PAIRS * i + j - behind < NQ

        def has(i, j, behind):
            return not isinstance(i, int) or PAIRS * i + j - behind >= 0

        def done(i, j, behind=0):
            return PAIRS * i + (j - behind + 1)

        def node_steps(engine, step):
            for b in range(RING):
                step(0, b)
            with engine.Fori(1, NG // RING) as i:
                for b in range(RING):
                    step(i, b)
            for g in range(NG // RING * RING, NG + 2):
                step(g // RING, g % RING)

        def group_alive(i, b, behind):
            return not isinstance(i, int) or 0 <= RING * i + b - behind < NG

        def group_has(i, b, behind):
            return not isinstance(i, int) or RING * i + b - behind >= 0

        def groups(i, b, behind=0):
            return RING * i + (b - behind + 1)

        @block.sync
        def _(sp):
            sp.dma_start(srcs[:], src_t).then_inc(tables_in, 16)
            sp.dma_start(dsts_i[:], dst_t).then_inc(tables_in, 16)
            sp.dma_start(shs[:].rearrange("p t m -> p (t m)"), sh_t).then_inc(tables_in, 16)
            sp.dma_start(wt[:], weights).then_inc(weights_in, 16)
            sp.dma_start(eas[:].rearrange("p b e -> p (b e)"), ea_t).then_inc(weights_in, 16)

            def load_rows(i, half):
                first = (i * BLOCK + half * 4) * P
                sp.dma_start(rows_now[:, half, :],
                             dst_rows[bass.ds(first, 4 * P)].partition_broadcast(P)
                             ).then_inc(rows_in[half], 16)

            for half in range(2):
                load_rows(0, half)
            sp.wait_ge(zeros_set, 1)
            for s in range(2):
                flat = acc[s].rearrange("(p r c) w -> p r (c w)", p=P, c=3)
                src = zeros[:].rearrange("p c w -> p (c w)").unsqueeze(1)
                sp.dma_start(flat, src.broadcast_to([P, ROWS // P // 3, 3 * AW])
                             ).then_inc(acc_zero, 16)
            for half in range(2):
                sp.wait_ge(same_ready, 2 * half + 2)
                load_rows(1, half)
            with sp.Fori(2, NB) as i:
                for half in range(2):
                    sp.wait_ge(same_ready, done(i - 1, 2 * half + 1))
                    load_rows(i, half)

            def x_rows(ap, g):
                return ap[bass.ds(g * (P * GROUP), P * GROUP), :].rearrange(
                    "(p k) w -> p (k w)", k=GROUP)

            for s in range(2):
                sp.wait_ge(added[s], 16 * NQ)

            def step(i, b):
                if group_alive(i, b, RING):
                    sp.wait_ge(fin_ready, groups(i, b, RING))
                    store_group(i, b, RING)
                if group_alive(i, b, 0):
                    g = RING * i + b
                    sp.dma_start(xin[:, b].rearrange("p k w -> p (k w)"),
                                 x_rows(table, g)).then_inc(x_in[b], 16)
                    for s in range(2):
                        sp.dma_start(acc_in[s][:, b].rearrange("p k w -> p (k w)"),
                                     x_rows(acc[s], g)).then_inc(acc_loaded[b], 16)

            def store_group(i, b, behind):
                sp.dma_start(x_rows(out, RING * i + (b - behind)),
                             fin[:, (b - behind) % 2].rearrange("p k w -> p (k w)")
                             ).then_inc(stored[(b - behind) % 2], 16)

            node_steps(sp, step)
            for g in range(NG + 2 - RING, NG):
                sp.wait_ge(fin_ready, g + 1)
                store_group(0, g, 0)
            for b in range(2):
                sp.wait_ge(stored[b], 16 * ((NG + 1 - b) // 2))

        @block.gpsimd
        def _(pool):
            nc.gpsimd.memset(zeros[:], 0.0).then_inc(zeros_set, 1)
            nc.gpsimd.iota(spare[:].bitcast(I32), pattern=[[0, T]], base=NP,
                           channel_multiplier=1).then_inc(spare_base, 1)
            nc.gpsimd.memset(ident[:], 0.0).then_inc(const_step, 1)
            nc.gpsimd.memset(later_mask[:], 1.0).then_inc(const_step, 1)
            nc.gpsimd.memset(eps[:], EPS).then_inc(const_ready, 1)
            nc.gpsimd.memset(msg[:], 1.0).then_inc(const_ready, 1)
            pool.wait_ge(const_step, 2)
            nc.gpsimd.affine_select(out=ident[:], in_=ident[:], compare_op=ALU.not_equal, fill=1.0,
                                    base=0, pattern=[[-1, P]], channel_multiplier=1
                                    ).then_inc(const_ready, 1)
            nc.gpsimd.affine_select(out=later_mask[:], in_=later_mask[:], compare_op=ALU.is_gt,
                                    fill=0.0, base=0, pattern=[[1, P]], channel_multiplier=-1
                                    ).then_inc(const_ready, 1)
            pool.wait_ge(tables_in, 48)

            def step(i, j):
                if alive(i, j, 0):
                    if j % 2 == 0:
                        for n in range(4):
                            if has(i, j, PAIRS):
                                pool.wait_ge(gathered[2 * j + n], 16 * i)
                        nc.gpsimd.tensor_copy(src_now[:, 2 * j:2 * j + 4],
                                              srcs[:, bass.ds(i * BLOCK + 2 * j, 4)]
                                              ).then_inc(src_ready, 1)
                        pool.wait_ge(src_ready, 2 * i + (j // 2 + 1))
                    if has(i, j, PAIRS):
                        pool.wait_ge(t_ready, done(i, j, PAIRS))
                    pool.sem_inc(gather_go, 1)
                    for n in (2 * j, 2 * j + 1):
                        pool.indirect_dma_start(
                            out=gat[:, n, 0:XW], out_offset=None, in_=table,
                            in_offset=bass.IndirectOffsetOnAxis(ap=src_now[:, n:n + 1], axis=0)
                        ).then_inc(gathered[n], 16)
                if alive(i, j, LAG):
                    if isinstance(i, int) and PAIRS * i + j == LAG:
                        pool.wait_ge(acc_zero, 32)
                    slot = (j - LAG) % PAIRS
                    pool.wait_ge(sums_ready, done(i, j, LAG))
                    pool.wait_ge(row_ready, done(i, j, LAG))
                    for s in range(2):
                        if has(i, j, LAG + 1):
                            pool.wait_ge(added[s], 16 * done(i, j, LAG + 1))
                        pool.sem_inc(scatter_go, 1)
                        pool.indirect_dma_start(
                            out=acc[s],
                            out_offset=bass.IndirectOffsetOnAxis(ap=row_now[:, slot, s:s + 1],
                                                                 axis=0),
                            in_=sums[:, slot, s, :], in_offset=None, compute_op=ALU.add
                        ).then_inc(added[s], 16)

            edge_steps(pool, step)

            def step(i, b):
                if group_alive(i, b, 0):
                    pool.wait_ge(acc_loaded[b], 32 * (i + 1))
                    if group_has(i, b, RING):
                        pool.wait_ge(res_ready, groups(i, b, RING))
                    nc.gpsimd.tensor_tensor(agg[:, b].rearrange("p k w -> p (k w)"),
                                            acc_in[0][:, b].rearrange("p k w -> p (k w)"),
                                            acc_in[1][:, b].rearrange("p k w -> p (k w)"),
                                            ALU.add).then_inc(agg_ready, 1)

            node_steps(pool, step)

        @block.tensor
        def _(pe):
            pe.wait_ge(weights_in, 32)
            pe.wait_ge(const_ready, 4)
            pe.wait_ge(wy_ready, 5)

            def step(i, j):
                b0, b1, b2 = j % 2, (j - 1) % 2, (j - 2) % 2
                if alive(i, j, 0):
                    if has(i, j, 1):
                        pe.wait_ge(t_out, done(i, j, 1))
                    pe.wait_ge(q_ready, done(i, j))
                    for c in range(2):
                        for s in range(2):
                            last = nc.tensor.transpose(
                                t_ps[:, c, s, :],
                                gat[:, 2 * j + s, 1 + c * MUL0:1 + c * MUL0 + P], ident[:])
                    last.then_inc(t_ready, 1)
                    if has(i, j, 1):
                        pe.wait_ge(h_out, done(i, j, 1))
                    nc.tensor.matmul(h_ps, wt[:, W_H + j * P:W_H + (j + 1) * P],
                                     eas[:, i, :] if isinstance(i, int)
                                     else eas[:, bass.ds(i, 1), :].squeeze(1),
                                     start=True, stop=True).then_inc(h_ready, 1)
                if alive(i, j, 1):
                    pe.wait_ge(t_out, done(i, j, 1))
                    if has(i, j, 2):
                        pe.wait_ge(e_out, done(i, j, 2))
                    for c, w in enumerate((W_E0, W_E1)):
                        last = nc.tensor.matmul(e_ps[:, c].rearrange("p s e -> p (s e)"),
                                                wt[:, w:w + P],
                                                t_sb[:, b1, c].rearrange("p s e -> p (s e)"),
                                                start=True, stop=True)
                    last.then_inc(e_ready, 1)
                    pe.wait_ge(h_out, done(i, j, 1))
                    if has(i, j, 2):
                        pe.wait_ge(mid_ready, done(i, j, 2))
                    for s in range(2):
                        for c in range(2):
                            w = W_W + (2 * s + c) * P
                            last = nc.tensor.matmul(w_ps[:, c, s, :], wt[:, w:w + P],
                                                    h_sb[:, b1, :], start=True, stop=True)
                    last.then_inc(w_ready, 1)
                if alive(i, j, 2):
                    pe.wait_ge(mid_ready, done(i, j, 2))
                    if has(i, j, 3):
                        pe.wait_ge(msg_ready, done(i, j, 3))
                    for s in range(2):
                        nc.tensor.matmul(y_ps[:, s, 0:W_Y1 - W_Y0], mid[:, b2, 0, s, :],
                                         wy[:, 0:W_Y1 - W_Y0], start=True, stop=True)
                        last = nc.tensor.matmul(y_ps[:, s, W_Y1 - W_Y0:YW], mid[:, b2, 1, s, :],
                                                wy[:, W_Y1 - W_Y0:W_S0 - W_Y0],
                                                start=True, stop=True)
                    last.then_inc(y_ready, 1)
                if alive(i, j, 3):
                    pe.wait_ge(msg_ready, done(i, j, 3))
                    pe.wait_ge(same_ready, done(i, j, 3))
                    if has(i, j, 5):
                        pe.wait_ge(sums_ready, done(i, j, 5))
                    for s in range(2):
                        last = nc.tensor.matmul(a_ps[:, b1, s, 0:AW], same[:, b1, s, :],
                                                msg[:, b1, s, :], start=True, stop=True)
                    last.then_inc(a_ready, 1)

            edge_steps(pe, step)

            def step(i, b):
                if group_alive(i, b, 0):
                    if group_has(i, b, 2):
                        pe.wait_ge(xt_out, groups(i, b, 2))
                    pe.wait_ge(x_in[b], 16 * (i + 1))
                    for c, n in ((0, P), (1, VEC)):
                        for k in range(GROUP):
                            last = nc.tensor.transpose(
                                xt_ps[0:n, b % 2, c, k, :],
                                xin[:, b, k, 1 + c * MUL0:1 + c * MUL0 + n], ident[:])
                    last.then_inc(xt_ready, 1)
                if group_alive(i, b, 1):
                    b1 = (b - 1) % 2
                    pe.wait_ge(xt_out, groups(i, b, 1))
                    if group_has(i, b, 3):
                        pe.wait_ge(pre_ready, groups(i, b, 3))
                    for k in range(GROUP):
                        nc.tensor.matmul(sc_ps[:, b1, k, 0:MUL0], xt[:, b1, 0, k, :],
                                         wy[:, W_S0 - W_Y0:W_S1 - W_Y0], start=True, stop=True)
                        last = nc.tensor.matmul(sc_ps[:, b1, k, MUL0:D], xt[0:VEC, b1, 1, k, :],
                                                wy[0:VEC, W_S1 - W_Y0:WC - W_Y0],
                                                start=True, stop=True)
                    last.then_inc(sc_ready, 1)

            pe.wait_ge(sums_ready, NQ)
            node_steps(pe, step)

        @block.scalar
        def _(act):
            def step(i, j):
                b0, b1, b2 = j % 2, (j - 1) % 2, (j - 2) % 2
                if alive(i, j, 0):
                    act.wait_ge(t_ready, done(i, j))
                    if has(i, j, 2):
                        act.wait_ge(e_ready, done(i, j, 2))
                    nc.scalar.activation(t_sb[:, b0].rearrange("p c s e -> p (c s e)"),
                                         t_ps.rearrange("p c s e -> p (c s e)"),
                                         ACT.Copy).then_inc(t_out, 1)
                    act.wait_ge(h_ready, done(i, j))
                    if has(i, j, 2):
                        act.wait_ge(w_ready, done(i, j, 2))
                    nc.scalar.activation(h_sb[:, b0, :], h_ps, ACT.Silu,
                                         scale=FC_IN ** -0.5).then_inc(h_out, 1)
                if alive(i, j, 1):
                    act.wait_ge(e_ready, done(i, j, 1))
                    if has(i, j, 3):
                        act.wait_ge(mid_ready, done(i, j, 3))
                    nc.scalar.activation(e_sb[:, b1].rearrange("p c s e -> p (c s e)"),
                                         e_ps.rearrange("p c s e -> p (c s e)"),
                                         ACT.Copy).then_inc(e_out, 1)
                if alive(i, j, 2):
                    act.wait_ge(y_ready, done(i, j, 2))
                    if has(i, j, 4):
                        act.wait_ge(msg_ready, done(i, j, 4))
                    nc.scalar.activation(z[:, b2, :, 0:1 + MUL0], y_ps[:, :, Y_C:YW],
                                         ACT.Copy).then_inc(zc_ready, 1)
                if alive(i, j, 3):
                    slot = (j - 3) % PAIRS
                    act.wait_ge(a_ready, done(i, j, 3))
                    if has(i, j, 3 + PAIRS):
                        for s in range(2):
                            act.wait_ge(added[s], 16 * done(i, j, 3 + PAIRS))
                    nc.scalar.activation(sums[:, slot], a_ps[:, b1, :, 0:AW],
                                         ACT.Copy).then_inc(sums_ready, 1)

            edge_steps(act, step)

            def step(i, b):
                b0 = b % 2
                if group_alive(i, b, 2):
                    act.wait_ge(mv_ready, groups(i, b, 2))
                    if group_has(i, b, 4):
                        act.wait_ge(rstd_ready, groups(i, b, 4))
                    nc.scalar.activation(std[:, b0], mv[:, b0, :, 1], ACT.Sqrt,
                                         bias=eps[:, 0:1]).then_inc(std_ready, 1)
                if group_alive(i, b, 0):
                    act.wait_ge(xt_ready, groups(i, b))
                    if group_has(i, b, 2):
                        act.wait_ge(sc_ready, groups(i, b, 2))
                    nc.scalar.activation(xt[:, b0, 0].rearrange("p k e -> p (k e)"),
                                         xt_ps[:, b0, 0].rearrange("p k e -> p (k e)"), ACT.Copy)
                    nc.scalar.activation(xt[0:VEC, b0, 1].rearrange("p k e -> p (k e)"),
                                         xt_ps[0:VEC, b0, 1].rearrange("p k e -> p (k e)"),
                                         ACT.Copy).then_inc(xt_out, 1)
                if group_alive(i, b, 2):
                    act.wait_ge(shift_ready, groups(i, b, 2))
                    if group_has(i, b, 4):
                        act.wait_ge(stored[b0], stored_before(i, b))
                    for k in range(GROUP):
                        last = nc.scalar.activation(fin[:, b0, k, :], res[:, b0, k, :],
                                                    ACT.Identity, bias=shift[:, b0, k:k + 1],
                                                    scale=rstd[:, b0, k:k + 1])
                    last.then_inc(fin_ready, 1)

            def stored_before(i, b):
                return 32 * i + 16 * (b // 2 - 1)

            node_steps(act, step)

        @block.vector
        def _(dve):
            dve.wait_ge(tables_in, 48)
            nc.vector.tensor_copy(dsts[:], dsts_i[:]).then_inc(dsts_ready, 1)
            dve.wait_ge(spare_base, 1)
            dve.wait_ge(dsts_ready, 1)
            nc.vector.tensor_tensor(spare[:], spare[:].bitcast(I32), dsts[:],
                                    ALU.subtract).then_inc(spare_ready, 1)
            dve.wait_ge(weights_in, 32)
            nc.vector.tensor_scalar(wy[:, 0:W_Y1 - W_Y0], wt[:, W_Y0:W_Y1], inv_fc * inv8 * inv96,
                                    None, ALU.mult).then_inc(wy_ready, 1)
            nc.vector.tensor_scalar(wy[0:VEC, W_Y1 - W_Y0:W_S0 - W_Y0], wt[0:VEC, W_Y1:W_S0],
                                    inv_fc * inv32 * inv96, None, ALU.mult).then_inc(wy_ready, 1)
            nc.vector.tensor_scalar(wy[VEC:P, W_Y1 - W_Y0:W_S0 - W_Y0], wt[VEC:P, W_Y1:W_S0],
                                    inv_fc * inv32 * inv96 * 3 ** -0.5, None,
                                    ALU.mult).then_inc(wy_ready, 1)
            nc.vector.tensor_scalar(wy[:, W_S0 - W_Y0:W_S1 - W_Y0], wt[:, W_S0:W_S1], inv8,
                                    None, ALU.mult).then_inc(wy_ready, 1)
            nc.vector.tensor_scalar(wy[:, W_S1 - W_Y0:WC - W_Y0], wt[:, W_S1:WC], inv32,
                                    None, ALU.mult).then_inc(wy_ready, 1)
            dve.wait_ge(const_ready, 4)
            dve.wait_ge(spare_ready, 1)

            def at(i, j):
                return bass.ds(i * BLOCK + 2 * j, 2)

            def step(i, j):
                b0, b1 = j % 2, (j - 1) % 2
                i2, j2 = (i, j - 2) if j >= 2 else (i - 1, j + 2)
                j3 = (j - 3) % PAIRS
                n = 2 * j
                if alive(i, j, 2):
                    half = j2 // 2
                    dve.wait_ge(rows_in[half], 16 * (i2 + 1))
                    if has(i, j, 4):
                        dve.wait_ge(a_ready, done(i, j, 4))
                        dve.wait_ge(later_ready, done(i, j, 4))
                    for s in range(2):
                        row = (2 * (j2 % 2) + s) * P
                        last = nc.vector.tensor_scalar(
                            same[:, b0, s, :], rows_now[:, half, row:row + P],
                            dsts[:, bass.ds(i2 * BLOCK + (2 * j2 + s), 1)], None, ALU.is_equal)
                    last.then_inc(same_ready, 1)
                if alive(i, j, 0):
                    if has(i, j, PAIRS):
                        dve.wait_ge(msg_ready, done(i, j, PAIRS))
                    for s in range(2):
                        dve.wait_ge(gathered[n + s], 16 * (i + 1))
                    nc.vector.tensor_tensor(sha[:, j], shs[:, at(i, j), :],
                                            gat[:, n:n + 2, 0:1].broadcast_to([P, 2, 4]),
                                            ALU.mult).then_inc(sha_ready, 1)
                if alive(i, j, 0):
                    if has(i, j, 1):
                        dve.wait_ge(q_ready, done(i, j, 1))
                    dve.wait_ge(sha_ready, done(i, j))
                    nc.vector.tensor_tensor(
                        qprod[:],
                        gat[:, n:n + 2, 1 + MUL0:XW].rearrange("p s (u m) -> p s u m", m=3),
                        sha[:, j, :, 1:4].unsqueeze(2).broadcast_to([P, 2, MUL1, 3]),
                        ALU.mult).then_inc(qprod_ready, 1)
                if alive(i, j, 2):
                    dve.wait_ge(same_ready, done(i, j, 2))
                    if has(i, j, 3):
                        dve.wait_ge(later_ready, done(i, j, 3))
                    if has(i, j, 4):
                        dve.wait_ge(moved_ready, done(i, j, 4))
                    for s in range(2):
                        last = nc.vector.tensor_tensor_reduce(
                            out=junk[:, s, :], in0=same[:, b0, s, :], in1=later_mask[:],
                            scale=1.0, scalar=0.0, op0=ALU.mult, op1=ALU.add,
                            accum_out=later[:, b0, s:s + 1])
                    last.then_inc(later_ready, 1)
                if alive(i, j, 0):
                    dve.wait_ge(qprod_ready, done(i, j))
                    nc.vector.tensor_reduce(gat[:, n:n + 2, QX:GW], qprod[:], AX_X,
                                            ALU.add).then_inc(q_ready, 1)
                if alive(i, j, 2):
                    dve.wait_ge(w_ready, done(i, j, 2))
                    dve.wait_ge(e_out, done(i, j, 2))
                    if has(i, j, 4):
                        dve.wait_ge(y_ready, done(i, j, 4))
                    nc.vector.tensor_tensor(mid[:, b0].rearrange("p c s e -> p (c s e)"),
                                            w_ps.rearrange("p c s e -> p (c s e)"),
                                            e_sb[:, b0].rearrange("p c s e -> p (c s e)"),
                                            ALU.mult).then_inc(mid_ready, 1)
                    dve.wait_ge(later_ready, done(i, j, 2))
                    if has(i, j, 4):
                        dve.wait_ge(row_ready, done(i, j, 4))
                    nc.vector.scalar_tensor_tensor(
                        out=moved[:, b0], in0=later[:, b0], scalar=1.0,
                        in1=spare[:, at(i2, j2)], op0=ALU.min, op1=ALU.mult
                    ).then_inc(moved_ready, 1)
                if alive(i, j, 3):
                    dve.wait_ge(zc_ready, done(i, j, 3))
                    if has(i, j, 5):
                        dve.wait_ge(msg_ready, done(i, j, 5))
                    nc.vector.tensor_tensor(
                        z[:, b1, :, 1 + MUL0:].rearrange("p s (v m) -> p s v m", m=3),
                        y_ps[:, :, Y_B:Y_B + MUL1].unsqueeze(3).broadcast_to([P, 2, MUL1, 3]),
                        sha[:, j3, :, 1:4].unsqueeze(2).broadcast_to([P, 2, MUL1, 3]),
                        ALU.mult).then_inc(zb_ready, 1)
                if alive(i, j, 2):
                    slot = j2
                    dve.wait_ge(moved_ready, done(i, j, 2))
                    if has(i, j, 2 + PAIRS):
                        for s in range(2):
                            dve.wait_ge(added[s], 16 * done(i, j, 2 + PAIRS))
                    nc.vector.tensor_tensor(row_now[:, slot, :], moved[:, b0],
                                            dsts[:, at(i2, j2)], ALU.add).then_inc(row_ready, 1)
                if alive(i, j, 3):
                    dve.wait_ge(zb_ready, done(i, j, 3))
                    if has(i, j, 5):
                        dve.wait_ge(a_ready, done(i, j, 5))
                    for s in range(2):
                        last = nc.vector.scalar_tensor_tensor(
                            out=msg[:, b1, s, 0:1 + D], in0=y_ps[:, s, Y_X:Y_C],
                            scalar=sha[:, j3, s, 0:1], in1=z[:, b1, s, :],
                            op0=ALU.mult, op1=ALU.add)
                    last.then_inc(msg_ready, 1)

            edge_steps(dve, step)

            def step(i, b):
                b1, b2 = (b - 1) % 2, b % 2
                slot = (b - 1) % RING
                if group_alive(i, b, 1):
                    g = groups(i, b, 1)
                    dve.wait_ge(agg_ready, g)
                    if group_has(i, b, 3):
                        dve.wait_ge(res_ready, groups(i, b, 3))
                    nc.vector.tensor_scalar(cnt[:, b1], agg[:, slot, :, CNT], 1.0, None,
                                            ALU.max).then_inc(cnt_ready, 1)
                    dve.wait_ge(sc_ready, g)
                    dve.wait_ge(x_in[slot], 16 * (g_round(i, b) + 1))
                    for k in range(GROUP):
                        if k == 1:
                            dve.wait_ge(cnt_ready, g)
                            nc.vector.reciprocal(rcnt[:, b1], cnt[:, b1]).then_inc(rcnt_ready, 1)
                        if k == 2:
                            dve.wait_ge(rcnt_ready, g)
                            nc.vector.tensor_tensor(ra[:, b1], rcnt[:, b1], xin[:, slot, :, 0],
                                                    ALU.mult).then_inc(ra_ready, 1)
                        if k == 3:
                            dve.wait_ge(ra_ready, g)
                            nc.vector.tensor_tensor(rr[:, b1], ra[:, b1], ra[:, b1],
                                                    ALU.mult).then_inc(rr_ready, 1)
                        last = nc.vector.scalar_tensor_tensor(
                            out=pre[:, b1, k, :], in0=sc_ps[:, b1, k, 0:D],
                            scalar=xin[:, slot, k, 0:1], in1=xin[:, slot, k, 1:XW],
                            op0=ALU.mult, op1=ALU.add)
                    last.then_inc(pre_ready, 1)
                    dve.wait_ge(rr_ready, g)
                    nc.vector.tensor_tensor(coef[:, b1], rr[:, b1], agg[:, slot, :, GATE],
                                            ALU.mult).then_inc(coef_ready, 1)
                if group_alive(i, b, 1):
                    dve.wait_ge(coef_ready, g)
                    if group_has(i, b, 3):
                        dve.wait_ge(fin_ready, groups(i, b, 3))
                    for k in range(GROUP):
                        last = nc.vector.scalar_tensor_tensor(
                            out=res[:, b1, k, :], in0=agg[:, slot, k, 1:1 + D],
                            scalar=coef[:, b1, k:k + 1], in1=pre[:, b1, k, :],
                            op0=ALU.mult, op1=ALU.add)
                    last.then_inc(res_ready, 1)
                    dve.wait_ge(res_ready, g)
                    if group_has(i, b, 3):
                        dve.wait_ge(shift_ready, groups(i, b, 3))
                    for k in range(GROUP):
                        last = nc.vector.bn_stats(stats[:, b1, k, :], res[:, b1, k, :])
                    last.then_inc(stats_ready, 1)
                    dve.wait_ge(stats_ready, g)
                if group_alive(i, b, 2):
                    g2 = groups(i, b, 2)
                    dve.wait_ge(std_ready, g2)
                    if group_has(i, b, 4):
                        dve.wait_ge(fin_ready, groups(i, b, 4))
                    nc.vector.reciprocal(rstd[:, b2], std[:, b2]).then_inc(rstd_ready, 1)
                    dve.wait_ge(rstd_ready, g2)
                    nc.vector.scalar_tensor_tensor(
                        out=shift[:, b2], in0=mv[:, b2, :, 0], scalar=-1.0, in1=rstd[:, b2],
                        op0=ALU.mult, op1=ALU.mult).then_inc(shift_ready, 1)
                if group_alive(i, b, 1):
                    for k in range(GROUP):
                        last = nc.vector.bn_aggr(mv[:, b1, k, :], stats[:, b1, k, :])
                    last.then_inc(mv_ready, 1)

            def g_round(i, b):
                return i + (b - 1) // RING

            node_steps(dve, step)


def pack_weights(np, Wfc1, Wfc2, Wsc0, Wsc1, Wl1_0, Wl1_1, Wl2_s, Wl2_v, Wa):
    w = np.zeros((P, WC), np.float32)
    for pair in range(PAIRS):
        for s in range(2):
            row = (2 * pair + s) * FC_IN
            col = W_H + pair * P + s * FC_H
            w[row:row + FC_IN, col:col + FC_H] = Wfc1
    for s in range(2):
        rows = slice(s * FC_H, (s + 1) * FC_H)
        col = W_W + 2 * s * P
        w[rows, col:col + P] = Wfc2[:, 0:P]
        for m in range(3):
            w[rows, col + P + m:col + P + VEC:3] = Wfc2[:, P:P + MUL1]
        w[rows, col + P + VEC:col + 2 * P] = Wfc2[:, P + MUL1:]
    for c in range(2):
        w[0:MUL0, W_E0 + c * MUL0:W_E0 + (c + 1) * MUL0] = Wl1_0
    for m in range(3):
        w[m:VEC:3, W_E1 + m:W_E1 + VEC:3] = Wl1_1
        w[m:VEC:3, W_Y1 + m:W_Y1 + VEC:3] = Wl2_v[MUL0:]
        w[m:VEC:3, W_S1 + m:W_S1 + VEC:3] = Wsc1
    w[VEC:P, W_E1 + VEC:W_E1 + P] = Wl1_1
    w[MUL0:P, W_Y0:W_Y0 + MUL1] = Wl2_v[:MUL0]
    w[0:MUL0, W_Y0 + MUL1] = Wa[:MUL0, 0]
    w[0:MUL0, W_Y0 + MUL1 + 1:W_Y1] = Wl2_s[:MUL0]
    w[VEC:P, W_Y1 + VEC] = Wa[MUL0:, 0]
    w[VEC:P, W_Y1 + VEC + 1:W_S0] = Wl2_s[MUL0:]
    w[0:MUL0, W_S0:W_S1] = Wsc0
    return w


def kernel(x, src, dst, edge_attr_16, edge_attr_4, node_vec1, **weights):
    import numpy as np
    import concourse.bacc as bacc
    from concourse.bass_utils import run_bass_kernel_spmd

    x, src, dst, ea, sh, a = (np.asarray(v) for v in
                              (x, src, dst, edge_attr_16, edge_attr_4, node_vec1))
    named = {k.removeprefix("L0_gnn_"): np.asarray(v) for k, v in weights.items()}
    N, E = x.shape[0], src.shape[0]
    NP = (N // (2 * GROUP * P) + 1) * 2 * GROUP * P
    T = -(-E // (BLOCK * P)) * BLOCK
    EP = T * P

    def rows(v, n, fill=0):
        return np.concatenate([v, np.full((n - v.shape[0],) + v.shape[1:], fill, v.dtype)])

    dst_p = rows(dst, EP, N)
    arrays = {
        "table": rows(np.concatenate([a, x], 1), NP),
        "src_t": np.ascontiguousarray(rows(src, EP).reshape(T, P).T),
        "dst_t": np.ascontiguousarray(dst_p.reshape(T, P).T),
        "dst_rows": dst_p,
        "sh_t": np.ascontiguousarray(
            rows(sh, EP).reshape(T, P, 4).transpose(1, 0, 2)).reshape(P, T * 4),
        "ea_t": np.ascontiguousarray(
            rows(ea, EP).reshape(T // BLOCK, BLOCK, P, FC_IN).transpose(1, 3, 0, 2)
        ).reshape(P, T // BLOCK * P),
        "weights": pack_weights(np, **named),
    }
    nc = bacc.Bacc("TRN2", target_bir_lowering=False, num_devices=1)
    args = [nc.dram_tensor(name, v.shape, mybir.dt.from_np(v.dtype), kind="ExternalInput").ap()
            for name, v in arrays.items()]
    out = nc.dram_tensor("out", (NP, D), F32, kind="ExternalOutput").ap()
    gnn_kernel(nc, *args, out)
    r = run_bass_kernel_spmd(nc, [arrays], core_ids=[0])
    return r.results[0]["out"][:N]
```

```python
from contextlib import ExitStack

import concourse.bass as bass
from concourse import mybir

P = 128
F32 = mybir.dt.float32
I32 = mybir.dt.int32
ALU = mybir.AluOpType
ACT = mybir.ActivationFunctionType
AX_X = mybir.AxisListType.X

MUL0, MUL1 = 64, 32
VEC = 3 * MUL1
D = MUL0 + VEC
FC_IN, FC_H = 16, 64
HID = MUL0 + MUL1
BLOCK = 8
PAIRS = BLOCK // 2
GROUP = 4
RING = 4
EPS = 1e-5

XW = 1 + D
QX = XW
GW = XW + MUL1
GATE, CNT, LABEL = 0, 1 + D, 2 + D
SW = 2 + D
AW = 3 + D
WINDOW = 2 * P
Y_B, Y_X, Y_C = 0, MUL1, MUL1 + 1 + D
YW = Y_C + 1 + MUL0

W_H = 0
W_W = W_H + PAIRS * P
W_E0 = W_W + 4 * P
W_E1 = W_E0 + P
W_Y0 = W_E1 + P
W_Y1 = W_Y0 + MUL1 + 1 + MUL0
W_S0 = W_Y1 + VEC + 1 + MUL0
W_S1 = W_S0 + MUL0
WC = W_S1 + VEC


def gnn_kernel(nc, table, src_t, dst_t, dst_rows, sh_t, ea_t, weights, out):
    NP = table.shape[0]
    T = src_t.shape[1]
    NB = T // BLOCK
    NQ = T // 2
    NG = NP // (P * GROUP)
    NT = NP // P
    EP = T * P
    BASE = EP + WINDOW
    ROWS = NP + P
    CH = 4
    assert NB > 2 and NG // RING > 1 and T <= 512 and NT < CH * P and ROWS % (3 * P) == 0

    inv8, inv32 = MUL0 ** -0.5, MUL1 ** -0.5
    inv96 = HID ** -0.5
    inv_fc = FC_H ** -0.5

    rows = nc.dram_tensor("rows", [BASE + ROWS, AW], F32, kind="Internal").ap()
    starts_dram = nc.dram_tensor("starts_dram", [CH * P], F32, kind="Internal").ap()

    with ExitStack() as ctx:
        def sb(name, shape, dt=F32):
            return ctx.enter_context(nc.sbuf_tensor(name, shape, dt))

        def sem(name):
            return ctx.enter_context(nc.semaphore(name))

        ps = ctx.enter_context(nc.psum_tensor("ps", [P, 8, 512], F32))
        wt = sb("wt", [P, WC])
        wy = sb("wy", [P, W_S1 + VEC - W_Y0])
        ident = sb("ident", [P, P])
        later_mask = sb("later_mask", [P, P])
        column = sb("column", [P, P])
        ones = sb("ones", [P, P])
        tile_base = sb("tile_base", [P, NT])
        srcs = sb("srcs", [P, T], I32)
        dsts_i = sb("dsts_i", [P, T], I32)
        dsts = sb("dsts", [P, T])
        shs = sb("shs", [P, T, 4])
        eas = sb("eas", [P, NB, P])
        zeros = sb("zeros", [P, 3, AW])
        pads = sb("pads", [P, 2, AW])

        heads_i = sb("heads_i", [1, T], I32)
        heads = sb("heads", [1, T])
        bound = sb("bound", [P, CH])
        seq = sb("seq", [P, 2, T], I32)
        greater = sb("greater", [P, T])
        wrong = sb("wrong", [P, 1])
        below = sb("below", [P, CH, T])
        tiles_below = sb("tiles_below", [P, CH])
        at_tile = sb("at_tile", [P, CH])
        at_tile_i = sb("at_tile_i", [P, CH], I32)
        picked = sb("picked", [P, CH, P], I32)
        picked_below = sb("picked_below", [P, CH, P])
        in_tile = sb("in_tile", [P, CH])
        starts = sb("starts", [P, CH])
        start_row = sb("start_row", [1, CH * P])
        node_base = sb("node_base", [1, NT])
        widths = sb("widths", [1, NT])
        widest = sb("widest", [1, 1])
        general = sb("general", [1, 1])
        general_i = sb("general_i", [1, 1], I32)
        moved_start = sb("moved_start", [1, NT])
        start_i = sb("start_i", [1, NT], I32)

        g_msg = sb("g_msg", [P, AW])
        g_dst = sb("g_dst", [P, P], I32)
        g_same = sb("g_same", [P, P])
        g_junk = sb("g_junk", [P, P])
        g_later = sb("g_later", [P, 1])
        g_spare = sb("g_spare", [P, 1])
        g_moved = sb("g_moved", [P, 1])
        g_row = sb("g_row", [P, 1], I32)
        g_sum = sb("g_sum", [P, AW])
        g_label = sb("g_label", [P, ROWS // P])

        src_now = sb("src_now", [P, BLOCK], I32)
        gat = sb("gat", [P, BLOCK, GW])
        sha = sb("sha", [P, PAIRS, 2, 4])
        qprod = sb("qprod", [P, 2, MUL1, 3])
        t_sb = sb("t_sb", [P, 2, 2, 2, P])
        h_sb = sb("h_sb", [P, 2, P])
        e_sb = sb("e_sb", [P, 2, 2, 2, P])
        mid = sb("mid", [P, 2, 2, 2, P])
        z = sb("z", [P, 2, 2, 1 + D])
        msg = sb("msg", [P, BLOCK, AW])

        xin = sb("xin", [P, RING, GROUP, XW])
        win = sb("win", [P, RING, GROUP, 2, AW])
        lab = sb("lab", [P, 2, GROUP, 2])
        hot = sb("hot", [P, 2, GROUP, 2, P])
        agg = sb("agg", [P, 2, GROUP, SW])
        xt = sb("xt", [P, 2, 2, GROUP, P])
        pre = sb("pre", [P, 2, GROUP, D])
        res = sb("res", [P, 2, GROUP, D])
        fin = sb("fin", [P, 2, GROUP, D])
        cnt = sb("cnt", [P, 2, GROUP])
        rcnt = sb("rcnt", [P, 2, GROUP])
        ra = sb("ra", [P, 2, GROUP])
        rr = sb("rr", [P, 2, GROUP])
        coef = sb("coef", [P, 2, GROUP])
        stats = sb("stats", [P, 2, GROUP, 6])
        mv = sb("mv", [P, 2, GROUP, 2])
        eps = sb("eps", [P, 1])
        std = sb("std", [P, 2, GROUP])
        rstd = sb("rstd", [P, 2, GROUP])
        shift = sb("shift", [P, 2, GROUP])

        t_ps = ps[:, 0, :].rearrange("p (c s e) -> p c s e", c=2, s=2)
        h_ps = ps[:, 1, 0:P]
        e_ps = ps[:, 2, :].rearrange("p (c s e) -> p c s e", c=2, s=2)
        w_ps = ps[:, 3, :].rearrange("p (c s e) -> p c s e", c=2, s=2)
        y_ps = ps[:, 4:6, :]
        heads_ps = ps[:, 6, 0:T]
        wrong_ps = ps[0:1, 7, 0:1]
        g_ps = ps[:, 7, 0:SW]
        xt_ps = ps[:, 0:2, :].rearrange("p c (k e) -> p c k e", k=GROUP)
        agg_ps = ps[:, 2:4, :].rearrange("p c (k e) -> p (c k) e", k=2)
        sc_ps = ps[:, 4:6, :].rearrange("p c (k e) -> p (c k) e", k=2)

        tables_in = sem("tables_in")
        weights_in = sem("weights_in")
        order_in = sem("order_in")
        consts_set = sem("consts_set")
        consts_ready = sem("consts_ready")
        iotas_set = sem("iotas_set")
        iotas_ready = sem("iotas_ready")
        pads_out = sem("pads_out")
        dsts_ready = sem("dsts_ready")
        wy_ready = sem("wy_ready")
        heads_ready = sem("heads_ready")
        heads_spread = sem("heads_spread")
        below_ready = sem("below_ready")
        tiles_below_ready = sem("tiles_below_ready")
        at_tile_ready = sem("at_tile_ready")
        at_tile_i_ready = sem("at_tile_i_ready")
        picked_in = sem("picked_in")
        picked_below_ready = sem("picked_below_ready")
        in_tile_ready = sem("in_tile_ready")
        starts_ready = sem("starts_ready")
        starts_out = sem("starts_out")
        starts_in = sem("starts_in")
        greater_ready = sem("greater_ready")
        wrong_ready = sem("wrong_ready")
        wrong_summed = sem("wrong_summed")
        widths_ready = sem("widths_ready")
        widest_ready = sem("widest_ready")
        over_ready = sem("over_ready")
        general_ready = sem("general_ready")
        moved_start_ready = sem("moved_start_ready")
        prepared = sem("prepared")
        src_ready = sem("src_ready")
        gathered = [sem(f"gathered{n}") for n in range(BLOCK)]
        gather_go = sem("gather_go")
        sha_ready = sem("sha_ready")
        qprod_ready = sem("qprod_ready")
        q_ready = sem("q_ready")
        t_ready = sem("t_ready")
        t_out = sem("t_out")
        h_ready = sem("h_ready")
        h_out = sem("h_out")
        e_ready = sem("e_ready")
        e_out = sem("e_out")
        w_ready = sem("w_ready")
        mid_ready = sem("mid_ready")
        y_ready = sem("y_ready")
        zc_ready = sem("zc_ready")
        zb_ready = sem("zb_ready")
        label_ready = sem("label_ready")
        msg_ready = sem("msg_ready")
        messages_out = [sem(f"messages_out{h}") for h in range(2)]

        g_zeroed = sem("g_zeroed")
        g_labelled = sem("g_labelled")
        g_loaded = sem("g_loaded")
        g_spare_ready = sem("g_spare_ready")
        g_same_ready = sem("g_same_ready")
        g_later_ready = sem("g_later_ready")
        g_moved_ready = sem("g_moved_ready")
        g_offset_ready = sem("g_offset_ready")
        g_row_ready = sem("g_row_ready")
        g_summed = sem("g_summed")
        g_sum_ready = sem("g_sum_ready")
        g_scatter_go = sem("g_scatter_go")
        g_added = sem("g_added")

        x_in = [sem(f"x_in{b}") for b in range(RING)]
        win_in = [sem(f"win_in{b}") for b in range(RING)]
        lab_ready = sem("lab_ready")
        hot_go = sem("hot_go")
        hot_ready = sem("hot_ready")
        agg_done = sem("agg_done")
        agg_ready = sem("agg_ready")
        xt_ready = sem("xt_ready")
        xt_out = sem("xt_out")
        sc_ready = sem("sc_ready")
        cnt_ready = sem("cnt_ready")
        rcnt_ready = sem("rcnt_ready")
        ra_ready = sem("ra_ready")
        rr_ready = sem("rr_ready")
        coef_ready = sem("coef_ready")
        pre_ready = sem("pre_ready")
        res_ready = sem("res_ready")
        stats_ready = sem("stats_ready")
        mv_ready = sem("mv_ready")
        std_ready = sem("std_ready")
        rstd_ready = sem("rstd_ready")
        shift_ready = sem("shift_ready")
        fin_ready = sem("fin_ready")
        stored = [sem(f"stored{b}") for b in range(2)]

        block = ctx.enter_context(nc.Block())

        def edge_steps(engine, step, prepare=None):
            for i in range(2):
                for j in range(PAIRS):
                    step(i, j)
                if i == 0 and prepare:
                    prepare()
            with engine.Fori(2, NB) as i:
                for j in range(PAIRS):
                    step(i, j)
            for j in range(3):
                step(NB, j)

        def alive(i, j, behind):
            return not isinstance(i, int) or 0 <= PAIRS * i + j - behind < NQ

        def has(i, j, behind):
            return not isinstance(i, int) or PAIRS * i + j - behind >= 0

        def done(i, j, behind=0):
            return PAIRS * i + (j - behind + 1)

        def node_steps(engine, step):
            for b in range(RING):
                step(0, b)
            with engine.Fori(1, NG // RING) as i:
                for b in range(RING):
                    step(i, b)
            for g in range(NG // RING * RING, NG + 2):
                step(g // RING, g % RING)

        def group_alive(i, b, behind):
            return not isinstance(i, int) or 0 <= RING * i + b - behind < NG

        def group_has(i, b, behind):
            return not isinstance(i, int) or RING * i + b - behind >= 0

        def groups(i, b, behind=0):
            return RING * i + (b - behind + 1)

        @block.sync
        def _(sp):
            sp.dma_start(srcs[:], src_t).then_inc(tables_in, 16)
            sp.dma_start(dsts_i[:], dst_t).then_inc(tables_in, 16)
            sp.dma_start(shs[:].rearrange("p t m -> p (t m)"), sh_t).then_inc(tables_in, 16)
            sp.dma_start(wt[:], weights).then_inc(weights_in, 16)
            sp.dma_start(eas[:].rearrange("p b e -> p (b e)"), ea_t).then_inc(weights_in, 16)
            with nc.allow_non_contiguous_dma("one number of each tile of edges, once"):
                sp.dma_start(heads_i[:].unsqueeze(2),
                             dst_rows[0:EP].rearrange("(o t p) -> o t p", o=1, p=P)[:, :, 0:1]
                             ).then_inc(order_in, 16)
            for n in range(2):
                sp.dma_start(seq[:, n, :], dst_rows[n:n + EP].rearrange("(p k) -> p k", p=P)
                             ).then_inc(order_in, 16)
            sp.wait_ge(consts_ready, 6)
            sp.dma_start(rows[EP:BASE, :].rearrange("(p c) w -> p (c w)", c=2),
                         pads[:].rearrange("p c w -> p (c w)")).then_inc(pads_out, 16)

            sp.wait_ge(starts_ready, 1)
            with nc.allow_non_contiguous_dma("one number of each tile of nodes, once"):
                sp.dma_start(starts_dram.rearrange("(c p o) -> p c o", p=P, o=1),
                             starts[:].unsqueeze(2)).then_inc(starts_out, 16)
            sp.wait_ge(starts_out, 16)
            sp.dma_start(start_row[:], starts_dram.rearrange("(o n) -> o n", o=1)
                         ).then_inc(starts_in, 16)

            with sp.Fori(0, NB) as i:
                for half in range(2):
                    sp.wait_ge(msg_ready, PAIRS * i + (2 * half + 2))
                    sp.dma_start(
                        rows[bass.ds(i * (BLOCK * P) + half * (4 * P), 4 * P), :].rearrange(
                            "(p n) w -> p (n w)", n=4),
                        msg[:, 4 * half:4 * half + 4, :].rearrange("p n w -> p (n w)")
                    ).then_inc(messages_out[half], 16)

            for half in range(2):
                sp.wait_ge(messages_out[half], 16 * NB)
            sp.wait_ge(pads_out, 16)
            sp.wait_ge(prepared, 1)

            with sp.If(sp.value_load(general_i[0:1, 0:1], min_val=0, max_val=1) != 0):
                own = rows[BASE:BASE + ROWS, :].rearrange("(p r) w -> p r w", p=P)
                sp.dma_start(own.rearrange("p (r c) w -> p r (c w)", c=3),
                             zeros[:].rearrange("p c w -> p (c w)").unsqueeze(1).broadcast_to(
                                 [P, ROWS // P // 3, 3 * AW])).then_inc(g_zeroed, 16)
                sp.wait_ge(g_zeroed, 16)
                with nc.allow_non_contiguous_dma("labels, in the general path"):
                    sp.dma_start(own[:, :, LABEL:AW], g_label[:].unsqueeze(2)
                                 ).then_inc(g_labelled, 16)
                sp.wait_ge(g_labelled, 16)

                def load_tile(t):
                    sp.dma_start(g_msg[:], rows[bass.ds(t * P, P), :]).then_inc(g_loaded, 16)
                    sp.dma_start(g_dst[:], dst_rows[bass.ds(t * P, P)].partition_broadcast(P)
                                 ).then_inc(g_loaded, 16)

                load_tile(0)
                with sp.Fori(1, T) as t:
                    sp.wait_ge(g_added, 16 * t)
                    load_tile(t)
                sp.wait_ge(g_added, 16 * T)

            def tile_rows(ap, i, b):
                first = (RING * i + b) * (P * GROUP)
                return ap[bass.ds(first, P * GROUP), :].rearrange("(k p) w -> p k w", k=GROUP)

            def store_group(i, b):
                sp.dma_start(tile_rows(out, i, b), fin[:, b % 2]).then_inc(stored[b % 2], 16)

            def step(i, b):
                if group_alive(i, b, RING):
                    sp.wait_ge(fin_ready, groups(i, b, RING))
                    store_group(i, b - RING)
                if group_alive(i, b, 0):
                    sp.dma_start(xin[:, b], tile_rows(table, i, b)).then_inc(x_in[b], 16)
                    for k in range(GROUP):
                        n = (RING * i + b) * GROUP + k
                        start = sp.value_load(start_i[0:1, bass.ds(n, 1)], min_val=0,
                                              max_val=BASE + NP - P)
                        sp.dma_start(win[:, b, k].rearrange("p c w -> p (c w)"),
                                     rows[bass.ds(start, WINDOW), :].rearrange(
                                         "(p c) w -> p (c w)", c=2)).then_inc(win_in[b], 16)

            node_steps(sp, step)
            for g in range(NG + 2 - RING, NG):
                sp.wait_ge(fin_ready, g + 1)
                store_group(0, g)
            for b in range(2):
                sp.wait_ge(stored[b], 16 * ((NG + 1 - b) // 2))

        @block.gpsimd
        def _(pool):
            for ap, pattern, base, mult in (
                    (column, [[1, P]], 0, 0), (tile_base, [[P, NT]], 0, 0),
                    (bound, [[P * P, CH]], 0, P), (node_base, [[P, NT]], BASE, 0),
                    (g_label, [[1, ROWS // P]], 0, ROWS // P), (g_spare, [[0, 1]], NP, 1)):
                nc.gpsimd.iota(ap[:].bitcast(I32), pattern=pattern, base=base,
                               channel_multiplier=mult).then_inc(iotas_set, 1)
            nc.gpsimd.memset(ident[:], 0.0).then_inc(consts_set, 1)
            nc.gpsimd.memset(later_mask[:], 1.0).then_inc(consts_set, 1)
            nc.gpsimd.memset(pads[:], 0.0).then_inc(consts_set, 1)
            nc.gpsimd.memset(msg[:], 1.0).then_inc(consts_ready, 1)
            nc.gpsimd.memset(ones[:], 1.0).then_inc(consts_ready, 1)
            nc.gpsimd.memset(eps[:], EPS).then_inc(consts_ready, 1)
            pool.wait_ge(consts_set, 3)
            nc.gpsimd.affine_select(out=ident[:], in_=ident[:], compare_op=ALU.not_equal, fill=1.0,
                                    base=0, pattern=[[-1, P]], channel_multiplier=1
                                    ).then_inc(consts_ready, 1)
            nc.gpsimd.affine_select(out=later_mask[:], in_=later_mask[:], compare_op=ALU.is_gt,
                                    fill=0.0, base=0, pattern=[[1, P]], channel_multiplier=-1
                                    ).then_inc(consts_ready, 1)
            nc.gpsimd.memset(pads[:, :, LABEL], -1.0).then_inc(consts_ready, 1)
            pool.wait_ge(tables_in, 48)

            def step(i, j):
                if not alive(i, j, 0):
                    return
                if j % 2 == 0:
                    for n in range(4):
                        if has(i, j, PAIRS):
                            pool.wait_ge(gathered[2 * j + n], 16 * i)
                    nc.gpsimd.tensor_copy(src_now[:, 2 * j:2 * j + 4],
                                          srcs[:, bass.ds(i * BLOCK + 2 * j, 4)]
                                          ).then_inc(src_ready, 1)
                    pool.wait_ge(src_ready, 2 * i + (j // 2 + 1))
                if has(i, j, PAIRS):
                    pool.wait_ge(t_ready, done(i, j, PAIRS))
                pool.sem_inc(gather_go, 1)
                for n in (2 * j, 2 * j + 1):
                    pool.indirect_dma_start(
                        out=gat[:, n, 0:XW], out_offset=None, in_=table,
                        in_offset=bass.IndirectOffsetOnAxis(ap=src_now[:, n:n + 1], axis=0)
                    ).then_inc(gathered[n], 16)

            def prepare():
                pool.wait_ge(at_tile_i_ready, 1)
                for c in range(CH):
                    pool.indirect_dma_start(
                        out=picked[:, c, :], out_offset=None,
                        in_=dst_rows.rearrange("(t p) -> t p", p=P),
                        in_offset=bass.IndirectOffsetOnAxis(ap=at_tile_i[:, c:c + 1], axis=0)
                    ).then_inc(picked_in, 16)

            edge_steps(pool, step, prepare)

            pool.wait_ge(prepared, 1)
            with pool.If(pool.value_load(general_i[0:1, 0:1], min_val=0, max_val=1) != 0):
                with pool.Fori(0, T) as t:
                    pool.wait_ge(g_sum_ready, t + 1)
                    pool.wait_ge(g_row_ready, t + 1)
                    pool.sem_inc(g_scatter_go, 1)
                    pool.indirect_dma_start(
                        out=rows, out_offset=bass.IndirectOffsetOnAxis(ap=g_row[:, 0:1], axis=0),
                        in_=g_sum[:], in_offset=None, compute_op=ALU.add).then_inc(g_added, 16)

            def node_step(i, b):
                if group_alive(i, b, 0):
                    b0 = b % 2
                    pool.wait_ge(win_in[b], 64 * (i + 1))
                    if group_has(i, b, 1):
                        pool.wait_ge(hot_ready, groups(i, b, 1))
                    nc.gpsimd.tensor_tensor(
                        lab[:, b0], win[:, b, :, :, LABEL],
                        tile_base[:, bass.ds((RING * i + b) * GROUP, GROUP)].unsqueeze(2)
                        .broadcast_to([P, GROUP, 2]), ALU.subtract).then_inc(lab_ready, 1)
                    pool.wait_ge(lab_ready, groups(i, b))
                    if group_has(i, b, 2):
                        pool.wait_ge(agg_done, groups(i, b, 2))
                    pool.sem_inc(hot_go, 1)
                    for k in range(GROUP):
                        for c in range(2):
                            last = nc.gpsimd.tensor_scalar(hot[:, b0, k, c, :], column[:],
                                                           lab[:, b0, k, c:c + 1], None,
                                                           ALU.is_equal)
                    last.then_inc(hot_ready, 1)

            node_steps(pool, node_step)

        @block.tensor
        def _(pe):
            pe.wait_ge(weights_in, 32)
            pe.wait_ge(consts_ready, 6)
            pe.wait_ge(wy_ready, 5)

            def step(i, j):
                b0, b1, b2 = j % 2, (j - 1) % 2, (j - 2) % 2
                if alive(i, j, 0):
                    if has(i, j, 1):
                        pe.wait_ge(t_out, done(i, j, 1))
                    pe.wait_ge(q_ready, done(i, j))
                    for c in range(2):
                        for s in range(2):
                            last = nc.tensor.transpose(
                                t_ps[:, c, s, :],
                                gat[:, 2 * j + s, 1 + c * MUL0:1 + c * MUL0 + P], ident[:])
                    last.then_inc(t_ready, 1)
                    if has(i, j, 1):
                        pe.wait_ge(h_out, done(i, j, 1))
                    nc.tensor.matmul(h_ps, wt[:, W_H + j * P:W_H + (j + 1) * P],
                                     eas[:, i, :] if isinstance(i, int)
                                     else eas[:, bass.ds(i, 1), :].squeeze(1),
                                     start=True, stop=True).then_inc(h_ready, 1)
                if alive(i, j, 1):
                    pe.wait_ge(t_out, done(i, j, 1))
                    if has(i, j, 2):
                        pe.wait_ge(e_out, done(i, j, 2))
                    for c, w in enumerate((W_E0, W_E1)):
                        last = nc.tensor.matmul(e_ps[:, c].rearrange("p s e -> p (s e)"),
                                                wt[:, w:w + P],
                                                t_sb[:, b1, c].rearrange("p s e -> p (s e)"),
                                                start=True, stop=True)
                    last.then_inc(e_ready, 1)
                    pe.wait_ge(h_out, done(i, j, 1))
                    if has(i, j, 2):
                        pe.wait_ge(mid_ready, done(i, j, 2))
                    for s in range(2):
                        for c in range(2):
                            w = W_W + (2 * s + c) * P
                            last = nc.tensor.matmul(w_ps[:, c, s, :], wt[:, w:w + P],
                                                    h_sb[:, b1, :], start=True, stop=True)
                    last.then_inc(w_ready, 1)
                if alive(i, j, 2):
                    pe.wait_ge(mid_ready, done(i, j, 2))
                    if has(i, j, 3):
                        pe.wait_ge(msg_ready, done(i, j, 3))
                    for s in range(2):
                        nc.tensor.matmul(y_ps[:, s, 0:W_Y1 - W_Y0], mid[:, b2, 0, s, :],
                                         wy[:, 0:W_Y1 - W_Y0], start=True, stop=True)
                        last = nc.tensor.matmul(y_ps[:, s, W_Y1 - W_Y0:YW], mid[:, b2, 1, s, :],
                                                wy[:, W_Y1 - W_Y0:W_S0 - W_Y0],
                                                start=True, stop=True)
                    last.then_inc(y_ready, 1)
            def prepare():
                pe.wait_ge(heads_ready, 1)
                nc.tensor.matmul(heads_ps, ones[0:1, :], heads[:], start=True,
                                 stop=True).then_inc(heads_spread, 1)
                pe.wait_ge(wrong_ready, 1)
                nc.tensor.matmul(wrong_ps, wrong[:], ones[:, 0:1], start=True,
                                 stop=True).then_inc(wrong_summed, 1)

            edge_steps(pe, step, prepare)

            pe.wait_ge(prepared, 1)
            with pe.If(pe.value_load(general_i[0:1, 0:1], min_val=0, max_val=1) != 0):
                with pe.Fori(0, T) as t:
                    pe.wait_ge(g_same_ready, t + 1)
                    nc.tensor.matmul(g_ps, g_same[:], g_msg[:, 0:SW], start=True,
                                     stop=True).then_inc(g_summed, 1)

            def step(i, b):
                if group_alive(i, b, 0):
                    if group_has(i, b, 1):
                        pe.wait_ge(xt_out, groups(i, b, 1))
                    pe.wait_ge(x_in[b], 16 * (i + 1))
                    for c, n in ((0, P), (1, VEC)):
                        for k in range(GROUP):
                            last = nc.tensor.transpose(
                                xt_ps[0:n, c, k, :],
                                xin[:, b, k, 1 + c * MUL0:1 + c * MUL0 + n], ident[:])
                    last.then_inc(xt_ready, 1)
                if group_alive(i, b, 1):
                    b1 = (b - 1) % 2
                    pe.wait_ge(hot_ready, groups(i, b, 1))
                    if group_has(i, b, 2):
                        pe.wait_ge(agg_ready, groups(i, b, 2))
                    for k in range(GROUP):
                        for c in range(2):
                            last = nc.tensor.matmul(agg_ps[:, k, 0:SW], hot[:, b1, k, c, :],
                                                    win[:, (b - 1) % RING, k, c, 0:SW],
                                                    start=c == 0, stop=c == 1)
                    last.then_inc(agg_done, 1)
                    pe.wait_ge(xt_out, groups(i, b, 1))
                    if group_has(i, b, 2):
                        pe.wait_ge(pre_ready, groups(i, b, 2))
                    for k in range(GROUP):
                        nc.tensor.matmul(sc_ps[:, k, 0:MUL0], xt[:, b1, 0, k, :],
                                         wy[:, W_S0 - W_Y0:W_S1 - W_Y0], start=True, stop=True)
                        last = nc.tensor.matmul(sc_ps[:, k, MUL0:D], xt[0:VEC, b1, 1, k, :],
                                                wy[0:VEC, W_S1 - W_Y0:WC - W_Y0],
                                                start=True, stop=True)
                    last.then_inc(sc_ready, 1)

            pe.wait_ge(msg_ready, NQ)
            node_steps(pe, step)

        @block.scalar
        def _(act):
            def step(i, j):
                b0, b1, b2 = j % 2, (j - 1) % 2, (j - 2) % 2
                if alive(i, j, 0):
                    act.wait_ge(t_ready, done(i, j))
                    if has(i, j, 2):
                        act.wait_ge(e_ready, done(i, j, 2))
                    nc.scalar.activation(t_sb[:, b0].rearrange("p c s e -> p (c s e)"),
                                         t_ps.rearrange("p c s e -> p (c s e)"),
                                         ACT.Copy).then_inc(t_out, 1)
                    act.wait_ge(h_ready, done(i, j))
                    if has(i, j, 2):
                        act.wait_ge(w_ready, done(i, j, 2))
                    nc.scalar.activation(h_sb[:, b0, :], h_ps, ACT.Silu,
                                         scale=FC_IN ** -0.5).then_inc(h_out, 1)
                if alive(i, j, 1):
                    act.wait_ge(e_ready, done(i, j, 1))
                    if has(i, j, 3):
                        act.wait_ge(mid_ready, done(i, j, 3))
                    nc.scalar.activation(e_sb[:, b1].rearrange("p c s e -> p (c s e)"),
                                         e_ps.rearrange("p c s e -> p (c s e)"),
                                         ACT.Copy).then_inc(e_out, 1)
                if alive(i, j, 2):
                    act.wait_ge(y_ready, done(i, j, 2))
                    if has(i, j, 4):
                        act.wait_ge(msg_ready, done(i, j, 4))
                    nc.scalar.activation(z[:, b2, :, 0:1 + MUL0], y_ps[:, :, Y_C:YW],
                                         ACT.Copy).then_inc(zc_ready, 1)
            edge_steps(act, step)

            def step(i, b):
                b0 = b % 2
                if group_alive(i, b, 2):
                    act.wait_ge(mv_ready, groups(i, b, 2))
                    if group_has(i, b, 4):
                        act.wait_ge(rstd_ready, groups(i, b, 4))
                    nc.scalar.activation(std[:, b0], mv[:, b0, :, 1], ACT.Sqrt,
                                         bias=eps[:, 0:1]).then_inc(std_ready, 1)
                if group_alive(i, b, 0):
                    act.wait_ge(xt_ready, groups(i, b))
                    if group_has(i, b, 2):
                        act.wait_ge(sc_ready, groups(i, b, 2))
                    nc.scalar.activation(xt[:, b0, 0].rearrange("p k e -> p (k e)"),
                                         xt_ps[:, 0].rearrange("p k e -> p (k e)"), ACT.Copy)
                    nc.scalar.activation(xt[0:VEC, b0, 1].rearrange("p k e -> p (k e)"),
                                         xt_ps[0:VEC, 1].rearrange("p k e -> p (k e)"),
                                         ACT.Copy).then_inc(xt_out, 1)
                if group_alive(i, b, 1):
                    act.wait_ge(agg_done, groups(i, b, 1))
                    if group_has(i, b, 3):
                        act.wait_ge(res_ready, groups(i, b, 3))
                    nc.scalar.activation(agg[:, 1 - b0], agg_ps[:, :, 0:SW],
                                         ACT.Copy).then_inc(agg_ready, 1)
                if group_alive(i, b, 2):
                    act.wait_ge(shift_ready, groups(i, b, 2))
                    if group_has(i, b, 4):
                        act.wait_ge(stored[b0], stored_before(i, b))
                    for k in range(GROUP):
                        last = nc.scalar.activation(fin[:, b0, k, :], res[:, b0, k, :],
                                                    ACT.Identity, bias=shift[:, b0, k:k + 1],
                                                    scale=rstd[:, b0, k:k + 1])
                    last.then_inc(fin_ready, 1)

            def stored_before(i, b):
                return 32 * i + 16 * (b // 2 - 1)

            node_steps(act, step)

        @block.vector
        def _(dve):
            dve.wait_ge(tables_in, 48)
            nc.vector.tensor_copy(dsts[:], dsts_i[:]).then_inc(dsts_ready, 1)
            dve.wait_ge(iotas_set, 6)
            for ap in (column, tile_base, bound, node_base, g_label, g_spare):
                nc.vector.tensor_copy(ap[:], ap[:].bitcast(I32)).then_inc(iotas_ready, 1)
            dve.wait_ge(weights_in, 32)
            nc.vector.tensor_scalar(wy[:, 0:W_Y1 - W_Y0], wt[:, W_Y0:W_Y1], inv_fc * inv8 * inv96,
                                    None, ALU.mult).then_inc(wy_ready, 1)
            nc.vector.tensor_scalar(wy[0:VEC, W_Y1 - W_Y0:W_S0 - W_Y0], wt[0:VEC, W_Y1:W_S0],
                                    inv_fc * inv32 * inv96, None, ALU.mult).then_inc(wy_ready, 1)
            nc.vector.tensor_scalar(wy[VEC:P, W_Y1 - W_Y0:W_S0 - W_Y0], wt[VEC:P, W_Y1:W_S0],
                                    inv_fc * inv32 * inv96 * 3 ** -0.5, None,
                                    ALU.mult).then_inc(wy_ready, 1)
            nc.vector.tensor_scalar(wy[:, W_S0 - W_Y0:W_S1 - W_Y0], wt[:, W_S0:W_S1], inv8,
                                    None, ALU.mult).then_inc(wy_ready, 1)
            nc.vector.tensor_scalar(wy[:, W_S1 - W_Y0:WC - W_Y0], wt[:, W_S1:WC], inv32,
                                    None, ALU.mult).then_inc(wy_ready, 1)
            nc.vector.memset(zeros[:], 0.0)
            nc.vector.memset(g_sum[:], 0.0)
            dve.wait_ge(consts_ready, 6)
            dve.wait_ge(dsts_ready, 1)
            dve.wait_ge(iotas_ready, 6)

            def at(i, j):
                return bass.ds(i * BLOCK + 2 * j, 2)

            def step(i, j):
                b0, b1 = j % 2, (j - 1) % 2
                i3 = i if j == 3 else i - 1
                j3 = (j - 3) % PAIRS
                n = 2 * j
                if alive(i, j, 0):
                    if has(i, j, PAIRS):
                        dve.wait_ge(msg_ready, done(i, j, PAIRS))
                    for s in range(2):
                        dve.wait_ge(gathered[n + s], 16 * (i + 1))
                    nc.vector.tensor_tensor(sha[:, j], shs[:, at(i, j), :],
                                            gat[:, n:n + 2, 0:1].broadcast_to([P, 2, 4]),
                                            ALU.mult).then_inc(sha_ready, 1)
                if alive(i, j, 0):
                    if has(i, j, 1):
                        dve.wait_ge(q_ready, done(i, j, 1))
                    dve.wait_ge(sha_ready, done(i, j))
                    nc.vector.tensor_tensor(
                        qprod[:],
                        gat[:, n:n + 2, 1 + MUL0:XW].rearrange("p s (u m) -> p s u m", m=3),
                        sha[:, j, :, 1:4].unsqueeze(2).broadcast_to([P, 2, MUL1, 3]),
                        ALU.mult).then_inc(qprod_ready, 1)
                if alive(i, j, 0):
                    dve.wait_ge(qprod_ready, done(i, j))
                    nc.vector.tensor_reduce(gat[:, n:n + 2, QX:GW], qprod[:], AX_X,
                                            ALU.add).then_inc(q_ready, 1)
                if alive(i, j, 2):
                    dve.wait_ge(w_ready, done(i, j, 2))
                    dve.wait_ge(e_out, done(i, j, 2))
                    if has(i, j, 4):
                        dve.wait_ge(y_ready, done(i, j, 4))
                    nc.vector.tensor_tensor(mid[:, b0].rearrange("p c s e -> p (c s e)"),
                                            w_ps.rearrange("p c s e -> p (c s e)"),
                                            e_sb[:, b0].rearrange("p c s e -> p (c s e)"),
                                            ALU.mult).then_inc(mid_ready, 1)
                if alive(i, j, 3):
                    dve.wait_ge(zc_ready, done(i, j, 3))
                    if has(i, j, 5):
                        dve.wait_ge(msg_ready, done(i, j, 5))
                    nc.vector.tensor_tensor(
                        z[:, b1, :, 1 + MUL0:].rearrange("p s (v m) -> p s v m", m=3),
                        y_ps[:, :, Y_B:Y_B + MUL1].unsqueeze(3).broadcast_to([P, 2, MUL1, 3]),
                        sha[:, j3, :, 1:4].unsqueeze(2).broadcast_to([P, 2, MUL1, 3]),
                        ALU.mult).then_inc(zb_ready, 1)
                if alive(i, j, 3):
                    if has(i, j, 3 + PAIRS):
                        dve.wait_ge(messages_out[j3 // 2], 16 * (i3 + 0))
                    nc.vector.tensor_copy(msg[:, 2 * j3:2 * j3 + 2, LABEL], dsts[:, at(i3, j3)]
                                          ).then_inc(label_ready, 1)
                if alive(i, j, 3):
                    dve.wait_ge(zb_ready, done(i, j, 3))
                    for s in range(2):
                        last = nc.vector.scalar_tensor_tensor(
                            out=msg[:, 2 * j3 + s, 0:1 + D], in0=y_ps[:, s, Y_X:Y_C],
                            scalar=sha[:, j3, s, 0:1], in1=z[:, b1, s, :],
                            op0=ALU.mult, op1=ALU.add)
                    last.then_inc(msg_ready, 1)

            def prepare():
                dve.wait_ge(order_in, 48)
                nc.vector.tensor_copy(heads[:], heads_i[:]).then_inc(heads_ready, 1)
                nc.vector.tensor_tensor(greater[:], seq[:, 0, :], seq[:, 1, :],
                                        ALU.is_gt).then_inc(greater_ready, 1)
                dve.wait_ge(greater_ready, 1)
                nc.vector.tensor_reduce(wrong[:], greater[:], AX_X, ALU.add
                                        ).then_inc(wrong_ready, 1)
                dve.wait_ge(heads_spread, 1)
                for c in range(CH):
                    last = nc.vector.tensor_scalar(below[:, c, :], heads_ps, bound[:, c:c + 1],
                                                   None, ALU.is_lt)
                last.then_inc(below_ready, 1)
                dve.wait_ge(below_ready, 1)
                nc.vector.tensor_reduce(tiles_below[:], below[:], AX_X, ALU.add
                                        ).then_inc(tiles_below_ready, 1)
                dve.wait_ge(tiles_below_ready, 1)
                nc.vector.tensor_scalar(at_tile[:], tiles_below[:], -1.0, 0.0, ALU.add, ALU.max
                                        ).then_inc(at_tile_ready, 1)
                dve.wait_ge(at_tile_ready, 1)
                nc.vector.tensor_copy(at_tile_i[:], at_tile[:]).then_inc(at_tile_i_ready, 1)
                dve.wait_ge(picked_in, 16 * CH)
                nc.vector.tensor_tensor(picked_below[:], picked[:],
                                        bound[:].unsqueeze(2).broadcast_to([P, CH, P]),
                                        ALU.is_lt).then_inc(picked_below_ready, 1)
                dve.wait_ge(picked_below_ready, 1)
                nc.vector.tensor_reduce(in_tile[:], picked_below[:], AX_X, ALU.add
                                        ).then_inc(in_tile_ready, 1)
                dve.wait_ge(in_tile_ready, 1)
                nc.vector.scalar_tensor_tensor(out=starts[:], in0=at_tile[:], scalar=float(P),
                                               in1=in_tile[:], op0=ALU.mult, op1=ALU.add
                                               ).then_inc(starts_ready, 1)
                dve.wait_ge(starts_in, 16)
                nc.vector.tensor_tensor(widths[:], start_row[:, 1:NT + 1], start_row[:, 0:NT],
                                        ALU.subtract).then_inc(widths_ready, 1)
                dve.wait_ge(widths_ready, 1)
                nc.vector.tensor_reduce(widest[:], widths[:], AX_X, ALU.max
                                        ).then_inc(widest_ready, 1)
                dve.wait_ge(widest_ready, 1)
                dve.wait_ge(wrong_summed, 1)
                nc.vector.scalar_tensor_tensor(out=general[:], in0=widest[:],
                                               scalar=float(WINDOW), in1=wrong_ps,
                                               op0=ALU.is_gt, op1=ALU.add
                                               ).then_inc(over_ready, 1)
                dve.wait_ge(over_ready, 1)
                nc.vector.tensor_scalar(general[:], general[:], 1.0, None, ALU.min
                                        ).then_inc(general_ready, 1)
                nc.vector.tensor_tensor(moved_start[:], node_base[:], start_row[:, 0:NT],
                                        ALU.subtract).then_inc(moved_start_ready, 1)
                dve.wait_ge(general_ready, 1)
                nc.vector.tensor_copy(general_i[:], general[:])
                dve.wait_ge(moved_start_ready, 1)
                nc.vector.scalar_tensor_tensor(out=start_i[:], in0=moved_start[:],
                                               scalar=general[:, 0:1],
                                               in1=start_row[:, 0:NT], op0=ALU.mult, op1=ALU.add
                                               ).then_inc(prepared, 1)

            edge_steps(dve, step, prepare)

            dve.wait_ge(prepared, 1)
            with dve.If(dve.value_load(general_i[0:1, 0:1], min_val=0, max_val=1) != 0):
                with dve.Fori(0, T) as t:
                    dve.wait_ge(g_loaded, 32 * t + 32)
                    nc.vector.tensor_scalar(g_same[:], g_dst[:], g_msg[:, LABEL:AW], None,
                                            ALU.is_equal).then_inc(g_same_ready, 1)
                    nc.vector.tensor_tensor(g_moved[:], g_spare[:], g_msg[:, LABEL:AW],
                                            ALU.subtract).then_inc(g_spare_ready, 1)
                    dve.wait_ge(g_same_ready, t + 1)
                    nc.vector.tensor_tensor(g_junk[:], g_same[:], later_mask[:], ALU.mult
                                            ).then_inc(g_later_ready, 1)
                    dve.wait_ge(g_later_ready, t + 1)
                    nc.vector.tensor_reduce(g_later[:], g_junk[:], AX_X, ALU.max
                                            ).then_inc(g_moved_ready, 1)
                    dve.wait_ge(g_moved_ready, t + 1)
                    dve.wait_ge(g_spare_ready, t + 1)
                    nc.vector.tensor_scalar(g_moved[:], g_moved[:], g_later[:, 0:1],
                                            float(BASE), ALU.mult, ALU.add
                                            ).then_inc(g_offset_ready, 1)
                    dve.wait_ge(g_offset_ready, t + 1)
                    nc.vector.tensor_tensor(g_row[:], g_moved[:], g_msg[:, LABEL:AW], ALU.add
                                            ).then_inc(g_row_ready, 1)
                    dve.wait_ge(g_summed, t + 1)
                    nc.vector.tensor_copy(g_sum[:, 0:SW], g_ps).then_inc(g_sum_ready, 1)

            def step(i, b):
                b1, b2 = (b - 1) % 2, b % 2
                slot = (b - 1) % RING
                if group_alive(i, b, 1):
                    g = groups(i, b, 1)
                    dve.wait_ge(agg_ready, g)
                    if group_has(i, b, 3):
                        dve.wait_ge(res_ready, groups(i, b, 3))
                    nc.vector.tensor_scalar(cnt[:, b1], agg[:, b1, :, CNT], 1.0, None,
                                            ALU.max).then_inc(cnt_ready, 1)
                    dve.wait_ge(sc_ready, g)
                    dve.wait_ge(x_in[slot], 16 * (g_round(i, b) + 1))
                    for k in range(GROUP):
                        if k == 1:
                            dve.wait_ge(cnt_ready, g)
                            nc.vector.reciprocal(rcnt[:, b1], cnt[:, b1]).then_inc(rcnt_ready, 1)
                        if k == 2:
                            dve.wait_ge(rcnt_ready, g)
                            nc.vector.tensor_tensor(ra[:, b1], rcnt[:, b1], xin[:, slot, :, 0],
                                                    ALU.mult).then_inc(ra_ready, 1)
                        if k == 3:
                            dve.wait_ge(ra_ready, g)
                            nc.vector.tensor_tensor(rr[:, b1], ra[:, b1], ra[:, b1],
                                                    ALU.mult).then_inc(rr_ready, 1)
                        last = nc.vector.scalar_tensor_tensor(
                            out=pre[:, b1, k, :], in0=sc_ps[:, k, 0:D],
                            scalar=xin[:, slot, k, 0:1], in1=xin[:, slot, k, 1:XW],
                            op0=ALU.mult, op1=ALU.add)
                    last.then_inc(pre_ready, 1)
                    dve.wait_ge(rr_ready, g)
                    nc.vector.tensor_tensor(coef[:, b1], rr[:, b1], agg[:, b1, :, GATE],
                                            ALU.mult).then_inc(coef_ready, 1)
                if group_alive(i, b, 1):
                    dve.wait_ge(coef_ready, g)
                    if group_has(i, b, 3):
                        dve.wait_ge(fin_ready, groups(i, b, 3))
                    for k in range(GROUP):
                        last = nc.vector.scalar_tensor_tensor(
                            out=res[:, b1, k, :], in0=agg[:, b1, k, 1:1 + D],
                            scalar=coef[:, b1, k:k + 1], in1=pre[:, b1, k, :],
                            op0=ALU.mult, op1=ALU.add)
                    last.then_inc(res_ready, 1)
                    dve.wait_ge(res_ready, g)
                    if group_has(i, b, 3):
                        dve.wait_ge(shift_ready, groups(i, b, 3))
                    for k in range(GROUP):
                        last = nc.vector.bn_stats(stats[:, b1, k, :], res[:, b1, k, :])
                    last.then_inc(stats_ready, 1)
                    dve.wait_ge(stats_ready, g)
                if group_alive(i, b, 2):
                    g2 = groups(i, b, 2)
                    dve.wait_ge(std_ready, g2)
                    if group_has(i, b, 4):
                        dve.wait_ge(fin_ready, groups(i, b, 4))
                    nc.vector.reciprocal(rstd[:, b2], std[:, b2]).then_inc(rstd_ready, 1)
                    dve.wait_ge(rstd_ready, g2)
                    nc.vector.scalar_tensor_tensor(
                        out=shift[:, b2], in0=mv[:, b2, :, 0], scalar=-1.0, in1=rstd[:, b2],
                        op0=ALU.mult, op1=ALU.mult).then_inc(shift_ready, 1)
                if group_alive(i, b, 1):
                    for k in range(GROUP):
                        last = nc.vector.bn_aggr(mv[:, b1, k, :], stats[:, b1, k, :])
                    last.then_inc(mv_ready, 1)

            def g_round(i, b):
                return i + (b - 1) // RING

            node_steps(dve, step)


def pack_weights(np, Wfc1, Wfc2, Wsc0, Wsc1, Wl1_0, Wl1_1, Wl2_s, Wl2_v, Wa):
    w = np.zeros((P, WC), np.float32)
    for pair in range(PAIRS):
        for s in range(2):
            row = (2 * pair + s) * FC_IN
            col = W_H + pair * P + s * FC_H
            w[row:row + FC_IN, col:col + FC_H] = Wfc1
    for s in range(2):
        rows = slice(s * FC_H, (s + 1) * FC_H)
        col = W_W + 2 * s * P
        w[rows, col:col + P] = Wfc2[:, 0:P]
        for m in range(3):
            w[rows, col + P + m:col + P + VEC:3] = Wfc2[:, P:P + MUL1]
        w[rows, col + P + VEC:col + 2 * P] = Wfc2[:, P + MUL1:]
    for c in range(2):
        w[0:MUL0, W_E0 + c * MUL0:W_E0 + (c + 1) * MUL0] = Wl1_0
    for m in range(3):
        w[m:VEC:3, W_E1 + m:W_E1 + VEC:3] = Wl1_1
        w[m:VEC:3, W_Y1 + m:W_Y1 + VEC:3] = Wl2_v[MUL0:]
        w[m:VEC:3, W_S1 + m:W_S1 + VEC:3] = Wsc1
    w[VEC:P, W_E1 + VEC:W_E1 + P] = Wl1_1
    w[MUL0:P, W_Y0:W_Y0 + MUL1] = Wl2_v[:MUL0]
    w[0:MUL0, W_Y0 + MUL1] = Wa[:MUL0, 0]
    w[0:MUL0, W_Y0 + MUL1 + 1:W_Y1] = Wl2_s[:MUL0]
    w[VEC:P, W_Y1 + VEC] = Wa[MUL0:, 0]
    w[VEC:P, W_Y1 + VEC + 1:W_S0] = Wl2_s[MUL0:]
    w[0:MUL0, W_S0:W_S1] = Wsc0
    return w


def kernel(x, src, dst, edge_attr_16, edge_attr_4, node_vec1, **weights):
    import numpy as np
    import concourse.bacc as bacc
    from concourse.bass_utils import run_bass_kernel_spmd

    x, src, dst, ea, sh, a = (np.asarray(v) for v in
                              (x, src, dst, edge_attr_16, edge_attr_4, node_vec1))
    named = {k.removeprefix("L0_gnn_"): np.asarray(v) for k, v in weights.items()}
    N, E = x.shape[0], src.shape[0]
    NP = (N // (GROUP * P) + 1) * GROUP * P
    T = -(-E // (BLOCK * P)) * BLOCK
    EP = T * P

    def rows(v, n, fill=0):
        return np.concatenate([v, np.full((n - v.shape[0],) + v.shape[1:], fill, v.dtype)])

    def tiles(v):
        v = v.reshape(T // 4, P, 4, -1).transpose(1, 0, 2, 3)
        return np.ascontiguousarray(v).reshape(P, -1)

    dst_p = rows(dst, EP, NP - 1)
    arrays = {
        "table": rows(np.concatenate([a, x], 1), NP),
        "src_t": tiles(rows(src, EP)),
        "dst_t": tiles(dst_p),
        "dst_rows": rows(dst, EP + P, NP - 1),
        "sh_t": tiles(rows(sh, EP)),
        "ea_t": np.ascontiguousarray(
            rows(ea, EP).reshape(T // BLOCK, 2, P, 4, FC_IN).transpose(1, 3, 4, 0, 2)
        ).reshape(P, T // BLOCK * P),
        "weights": pack_weights(np, **named),
    }
    nc = bacc.Bacc("TRN2", target_bir_lowering=False, num_devices=1)
    args = [nc.dram_tensor(name, v.shape, mybir.dt.from_np(v.dtype), kind="ExternalInput").ap()
            for name, v in arrays.items()]
    out = nc.dram_tensor("out", (NP, D), F32, kind="ExternalOutput").ap()
    gnn_kernel(nc, *args, out)
    r = run_bass_kernel_spmd(nc, [arrays], core_ids=[0])
    return r.results[0]["out"][:N]
```

```python
from contextlib import ExitStack

import concourse.bass as bass
from concourse import mybir

P = 128
F32 = mybir.dt.float32
I32 = mybir.dt.int32
ALU = mybir.AluOpType
ACT = mybir.ActivationFunctionType
AX_X = mybir.AxisListType.X

MUL0, MUL1 = 64, 32
VEC = 3 * MUL1
D = MUL0 + VEC
FC_IN, FC_H = 16, 64
HID = MUL0 + MUL1
BLOCK = 8
PAIRS = BLOCK // 2
GROUP = 4
RING = 4
REST = 6
EPS = 1e-5

XW = 1 + D
QX = XW
GW = XW + MUL1
GATE, CNT, LABEL = 0, 1 + D, 2 + D
SW = 2 + D
AW = 3 + D
WP = 96
WINDOW = 2 * WP
Y_C = 1 + D
YW = Y_C + 1 + MUL0

W_H = 0
W_W = W_H + PAIRS * P
W_E0 = W_W + 4 * P
W_E1 = W_E0 + P
W_Y0 = W_E1 + P
W_YB = W_Y0 + 2 * (1 + MUL0)
W_Y1 = W_YB + 2 * MUL1
W_S0 = W_Y1 + VEC + 1 + MUL0
W_S1 = W_S0 + 2 * MUL0
WC = W_S1 + VEC


def gnn_kernel(nc, table, src_t, dst_t, dst_rows, sh_t, ea_t, weights, out):
    NP = table.shape[0]
    T = src_t.shape[1]
    NB = T // BLOCK
    NQ = T // 2
    NG = NP // (P * GROUP)
    NT = NP // P
    EP = T * P
    BASE = EP + WINDOW
    ROWS = NP + P
    FILL = max(f for f in range(1, 9) if ROWS // P % f == 0)
    CH = 4
    assert NB > 2 and NG // RING > 2 and NG % 2 == 0 and T <= 512 and NT < CH * P 

    inv8, inv32 = MUL0 ** -0.5, MUL1 ** -0.5
    inv96 = HID ** -0.5
    inv_fc = FC_H ** -0.5

    rows = nc.dram_tensor("rows", [BASE + ROWS, AW], F32, kind="Internal").ap()
    starts_dram = nc.dram_tensor("starts_dram", [CH * P], F32, kind="Internal").ap()

    with ExitStack() as ctx:
        def sb(name, shape, dt=F32):
            return ctx.enter_context(nc.sbuf_tensor(name, shape, dt))

        def sem(name):
            return ctx.enter_context(nc.semaphore(name))

        ps = ctx.enter_context(nc.psum_tensor("ps", [P, 8, 512], F32))
        wt = sb("wt", [P, WC])
        wy = sb("wy", [P, W_S1 + VEC - W_Y0])
        ident = sb("ident", [P, P])
        later_mask = sb("later_mask", [P, P])
        column = sb("column", [P, P])
        ones = sb("ones", [P, P])
        tile_base = sb("tile_base", [P, NT])
        srcs = sb("srcs", [P, T], I32)
        dsts_i = sb("dsts_i", [P, T], I32)
        dsts = sb("dsts", [P, T])
        shs = sb("shs", [P, T, 4])
        eas = sb("eas", [P, NB, P])
        zeros = sb("zeros", [P, FILL, AW])
        pads = sb("pads", [WP, 2, AW])

        heads_i = sb("heads_i", [1, T], I32)
        heads = sb("heads", [1, T])
        bound = sb("bound", [P, CH])
        seq = sb("seq", [P, 2, T], I32)
        greater = sb("greater", [P, T])
        wrong = sb("wrong", [P, 1])
        below = sb("below", [P, CH, T])
        tiles_below = sb("tiles_below", [P, CH])
        at_tile = sb("at_tile", [P, CH])
        at_tile_i = sb("at_tile_i", [P, CH], I32)
        picked = sb("picked", [P, CH, P], I32)
        picked_below = sb("picked_below", [P, CH, P])
        in_tile = sb("in_tile", [P, CH])
        starts = sb("starts", [P, CH])
        start_row = sb("start_row", [1, CH * P])
        node_base = sb("node_base", [1, NT])
        widths = sb("widths", [1, NT])
        widest = sb("widest", [1, 1])
        general = sb("general", [1, 1])
        general_i = sb("general_i", [1, 1], I32)
        moved_start = sb("moved_start", [1, NT])
        start_i = sb("start_i", [1, NT], I32)

        g_msg = sb("g_msg", [P, AW])
        g_dst = sb("g_dst", [P, P], I32)
        g_same = sb("g_same", [P, P])
        g_junk = sb("g_junk", [P, P])
        g_later = sb("g_later", [P, 1])
        g_spare = sb("g_spare", [P, 1])
        g_moved = sb("g_moved", [P, 1])
        g_row = sb("g_row", [P, 1], I32)
        g_sum = sb("g_sum", [P, AW])
        g_label = sb("g_label", [P, ROWS // P])

        src_now = sb("src_now", [P, BLOCK], I32)
        gat = sb("gat", [P, BLOCK, GW])
        sha = sb("sha", [P, PAIRS, 2, 4])
        x0 = sb("x0", [P, 2, 2, MUL0])
        qprod = sb("qprod", [P, 2, MUL1, 3])
        t_sb = sb("t_sb", [P, 2, 3, P])
        h_sb = sb("h_sb", [P, 2, P])
        e_sb = sb("e_sb", [P, 2, 3, P])
        mid = sb("mid", [P, 2, 4, P])
        z = sb("z", [P, 2, 2, 1 + D])
        msg = sb("msg", [P, BLOCK, AW])

        xin = sb("xin", [P, RING, GROUP, XW])
        win = sb("win", [WP, RING, GROUP, 2, AW])
        xa0 = sb("xa0", [P, 2, GROUP, MUL0])
        xa1 = sb("xa1", [P, 2, GROUP, VEC])
        lab = sb("lab", [WP, 2, GROUP, 2])
        hot = sb("hot", [WP, 2, GROUP, 2, P])
        agg = sb("agg", [P, 2, GROUP, D])
        xt0 = sb("xt0", [P, 2, GROUP // 2, P])
        xt1 = sb("xt1", [VEC, 2, GROUP, P])
        pre = sb("pre", [P, 2, GROUP, D])
        res = sb("res", [P, RING, GROUP, D])
        fin = sb("fin", [P, RING, GROUP, D])
        cnt = sb("cnt", [P, 2, GROUP])
        rcnt = sb("rcnt", [P, 2, GROUP])
        ra = sb("ra", [P, 2, GROUP])
        rr = sb("rr", [P, 2, GROUP])
        coef = sb("coef", [P, 2, GROUP])
        stats = sb("stats", [P, RING, GROUP, 6])
        mv = sb("mv", [P, RING, GROUP, 2])
        eps = sb("eps", [P, 1])
        std = sb("std", [P, RING, GROUP])
        rstd = sb("rstd", [P, RING, GROUP])
        shift = sb("shift", [P, RING, GROUP])

        t_ps = ps[:, 0, 0:3 * P].rearrange("p (c e) -> p c e", e=P)
        h_ps = ps[:, 1, 0:P]
        e_ps = ps[:, 2, 0:3 * P].rearrange("p (c e) -> p c e", e=P)
        w_ps = ps[:, 3, :].rearrange("p (c e) -> p c e", e=P)
        y_ps = ps[:, 4, 0:2 * YW].rearrange("p (s w) -> p s w", s=2)
        yb_ps = ps[:, 5, 0:2 * MUL1].rearrange("p (s w) -> p s w", s=2)
        heads_ps = ps[:, 6, 0:T]
        wrong_ps = ps[0:1, 7, 0:1]
        g_ps = ps[:, 7, 0:SW]
        xt0_ps = ps[:, 0, 0:GROUP // 2 * P].rearrange("p (k e) -> p k e", e=P)
        xt1_ps = ps[0:VEC, 1, :].rearrange("p (k e) -> p k e", k=GROUP)
        agg_ps = [ps[:, n:n + 2, :].rearrange("p c (k e) -> p (c k) e", k=2) for n in (2, 6)]
        sc0_ps = ps[:, 4:6, 0:2 * MUL0]
        sc1_ps = ps[:, 4:6, 2 * MUL0:2 * D]

        srcs_in = sem("srcs_in")
        tables_in = sem("tables_in")
        rest_in = sem("rest_in")
        weights_in = sem("weights_in")
        order_in = sem("order_in")
        consts_set = sem("consts_set")
        consts_ready = sem("consts_ready")
        iotas_set = sem("iotas_set")
        iotas_ready = sem("iotas_ready")
        table_ready = sem("table_ready")
        mask_ready = sem("mask_ready")
        zeros_set = sem("zeros_set")
        pads_set = sem("pads_set")
        pads_ready = sem("pads_ready")
        pads_out = sem("pads_out")
        dsts_ready = sem("dsts_ready")
        wy_ready = sem("wy_ready")
        heads_ready = sem("heads_ready")
        heads_spread = sem("heads_spread")
        below_ready = sem("below_ready")
        tiles_below_ready = sem("tiles_below_ready")
        at_tile_ready = sem("at_tile_ready")
        at_tile_i_ready = sem("at_tile_i_ready")
        picked_in = sem("picked_in")
        picked_below_ready = sem("picked_below_ready")
        in_tile_ready = sem("in_tile_ready")
        starts_ready = sem("starts_ready")
        starts_out = sem("starts_out")
        starts_in = sem("starts_in")
        greater_ready = sem("greater_ready")
        wrong_ready = sem("wrong_ready")
        wrong_summed = sem("wrong_summed")
        widths_ready = sem("widths_ready")
        widest_ready = sem("widest_ready")
        over_ready = sem("over_ready")
        general_ready = sem("general_ready")
        moved_start_ready = sem("moved_start_ready")
        prepared = sem("prepared")
        src_ready = sem("src_ready")
        gathered = [sem(f"gathered{n}") for n in range(BLOCK)]
        gather_go = sem("gather_go")
        sha_ready = sem("sha_ready")
        qprod_ready = sem("qprod_ready")
        q_ready = sem("q_ready")
        t_ready = sem("t_ready")
        t_out = sem("t_out")
        h_ready = sem("h_ready")
        h_out = sem("h_out")
        e_ready = sem("e_ready")
        e_out = sem("e_out")
        w_ready = sem("w_ready")
        mid_ready = sem("mid_ready")
        y_ready = sem("y_ready")
        zc_ready = sem("zc_ready")
        zb_ready = sem("zb_ready")
        label_ready = sem("label_ready")
        msg_ready = sem("msg_ready")
        messages_out = [sem(f"messages_out{h}") for h in range(2)]

        g_zeroed = sem("g_zeroed")
        g_labelled = sem("g_labelled")
        g_loaded = sem("g_loaded")
        g_spare_ready = sem("g_spare_ready")
        g_same_ready = sem("g_same_ready")
        g_later_ready = sem("g_later_ready")
        g_moved_ready = sem("g_moved_ready")
        g_offset_ready = sem("g_offset_ready")
        g_row_ready = sem("g_row_ready")
        g_summed = sem("g_summed")
        g_sum_ready = sem("g_sum_ready")
        g_scatter_go = sem("g_scatter_go")
        g_added = sem("g_added")

        x_in = [sem(f"x_in{b}") for b in range(RING)]
        win_in = [sem(f"win_in{b}") for b in range(RING)]
        xa_ready = sem("xa_ready")
        lab_ready = sem("lab_ready")
        hot_ready = sem("hot_ready")
        agg_done = sem("agg_done")
        agg_ready = sem("agg_ready")
        xt_ready = sem("xt_ready")
        xt_out = sem("xt_out")
        sc_ready = sem("sc_ready")
        cnt_ready = sem("cnt_ready")
        rcnt_ready = sem("rcnt_ready")
        ra_ready = sem("ra_ready")
        rr_ready = sem("rr_ready")
        coef_ready = sem("coef_ready")
        pre_ready = sem("pre_ready")
        res_ready = sem("res_ready")
        stats_ready = sem("stats_ready")
        aggr_go = sem("aggr_go")
        mv_ready = sem("mv_ready")
        std_ready = sem("std_ready")
        rstd_ready = sem("rstd_ready")
        shift_ready = sem("shift_ready")
        fin_ready = sem("fin_ready")
        stored = [sem(f"stored{b}") for b in range(2)]

        block = ctx.enter_context(nc.Block())

        def edge_steps(engine, step, between={}):
            for i in range(2):
                for j in range(PAIRS):
                    step(i, j)
                    if (i, j) in between:
                        between[i, j]()
            with engine.Fori(2, NB) as i:
                for j in range(PAIRS):
                    step(i, j)
            if NB in between:
                between[NB]()
            for j in range(3):
                step(NB, j)

        def alive(i, j, behind):
            return not isinstance(i, int) or 0 <= PAIRS * i + j - behind < NQ

        def has(i, j, behind):
            return not isinstance(i, int) or PAIRS * i + j - behind >= 0

        def done(i, j, behind=0):
            return PAIRS * i + (j - behind + 1)

        def node_steps(engine, step):
            for g in range(2 * RING):
                step(g // RING, g % RING)
            with engine.Fori(2, NG // RING) as i:
                for b in range(RING):
                    step(i, b)
            for g in range(NG // RING * RING, NG + 8):
                step(g // RING, g % RING)

        def group_alive(i, b, behind):
            return not isinstance(i, int) or 0 <= RING * i + b - behind < NG

        def group_has(i, b, behind):
            return not isinstance(i, int) or RING * i + b - behind >= 0

        def groups(i, b, behind=0):
            return RING * i + (b - behind + 1)

        def tile_rows(ap, i, b, n=1):
            first = (RING * i + b) * (P * GROUP)
            return ap[bass.ds(first, n * P * GROUP), :].rearrange("(k p) w -> p k w", p=P)

        @block.sync
        def _(sp):
            first = slice(0, 2 * BLOCK * 4), slice(0, 2 * P)
            rest = slice(2 * BLOCK * 4, T * 4)
            sh_all = shs[:].rearrange("p t m -> p (t m)")
            ea_all = eas[:].rearrange("p b e -> p (b e)")
            sp.dma_start(srcs[:], src_t).then_inc(srcs_in, 16)
            sp.dma_start(wt[:], weights).then_inc(weights_in, 16)
            sp.dma_start(ea_all[:, first[1]], ea_t[:, first[1]]).then_inc(weights_in, 16)
            sp.dma_start(sh_all[:, first[0]], sh_t[:, first[0]]).then_inc(tables_in, 16)
            sp.dma_start(dsts_i[:], dst_t).then_inc(tables_in, 16)
            with nc.allow_non_contiguous_dma("one number of each tile of edges, once"):
                sp.dma_start(heads_i[:].unsqueeze(2),
                             dst_rows[0:EP].rearrange("(o t p) -> o t p", o=1, p=P)[:, :, 0:1]
                             ).then_inc(order_in, 16)
            for n in range(2):
                sp.dma_start(seq[:, n, :], dst_rows[n:n + EP].rearrange("(p k) -> p k", p=P)
                             ).then_inc(order_in, 16)
            sp.wait_ge(gathered[BLOCK - 1], 16)
            sp.dma_start(sh_all[:, rest], sh_t[:, rest]).then_inc(rest_in, 16)
            for n in range(REST):
                part = slice((2 + (NB - 2) * n // REST) * P, (2 + (NB - 2) * (n + 1) // REST) * P)
                sp.dma_start(ea_all[:, part], ea_t[:, part]).then_inc(rest_in, 16)
            sp.wait_ge(pads_ready, 1)
            sp.dma_start(rows[EP:BASE, :].rearrange("(p c) w -> p (c w)", c=2),
                         pads[:].rearrange("p c w -> p (c w)")).then_inc(pads_out, 16)

            def store_messages(i):
                for half in range(2):
                    sp.wait_ge(msg_ready, PAIRS * i + (2 * half + 2))
                    sp.dma_start(
                        rows[bass.ds(i * (BLOCK * P) + half * (4 * P), 4 * P), :].rearrange(
                            "(p n) w -> p (n w)", n=4),
                        msg[:, 4 * half:4 * half + 4, :].rearrange("p n w -> p (n w)")
                    ).then_inc(messages_out[half], 16)

            store_messages(0)
            sp.wait_ge(starts_ready, 1)
            with nc.allow_non_contiguous_dma("one number of each tile of nodes, once"):
                sp.dma_start(starts_dram.rearrange("(c p o) -> p c o", p=P, o=1),
                             starts[:].unsqueeze(2)).then_inc(starts_out, 16)
            sp.wait_ge(starts_out, 16)
            sp.dma_start(start_row[:], starts_dram.rearrange("(o n) -> o n", o=1)
                         ).then_inc(starts_in, 16)
            for b in range(RING):
                sp.dma_start(xin[:, b], tile_rows(table, 0, b)).then_inc(x_in[b], 16)
            with sp.Fori(1, NB) as i:
                store_messages(i)

            sp.wait_ge(prepared, 1)
            is_general = sp.value_load(general_i[0:1, 0:1], min_val=0, max_val=1)
            for half in range(2):
                sp.wait_ge(messages_out[half], 16 * NB)
            sp.wait_ge(pads_out, 16)
            with sp.If(is_general != 0):
                sp.wait_ge(zeros_set, 2)
                own = rows[BASE:BASE + ROWS, :].rearrange("(p r) w -> p r w", p=P)
                sp.dma_start(own.rearrange("p (r c) w -> p r (c w)", c=FILL),
                             zeros[:].rearrange("p c w -> p (c w)").unsqueeze(1).broadcast_to(
                                 [P, ROWS // P // FILL, FILL * AW])).then_inc(g_zeroed, 16)
                sp.wait_ge(g_zeroed, 16)
                with nc.allow_non_contiguous_dma("labels, in the general path"):
                    sp.dma_start(own[:, :, LABEL:AW], g_label[:].unsqueeze(2)
                                 ).then_inc(g_labelled, 16)
                sp.wait_ge(g_labelled, 16)

                def load_tile(t):
                    sp.dma_start(g_msg[:], rows[bass.ds(t * P, P), :]).then_inc(g_loaded, 16)
                    sp.dma_start(g_dst[:], dst_rows[bass.ds(t * P, P)].partition_broadcast(P)
                                 ).then_inc(g_loaded, 16)

                load_tile(0)
                with sp.Fori(1, T) as t:
                    sp.wait_ge(g_added, 16 * t)
                    load_tile(t)
                sp.wait_ge(g_added, 16 * T)

            def step(i, b):
                if group_alive(i, b, 0):
                    _, firsts = nc.values_load_multi_w_load_instructions(
                        start_i[0:1, bass.ds((RING * i + b) * GROUP, GROUP)],
                        engines=[mybir.EngineType.SP], min_val=0, max_val=BASE + NP - P,
                        skip_runtime_bounds_check_because="a start is a count of edges, or the first "
                        "of a tile's own rows")
                    if group_has(i, b, RING):
                        sp.wait_ge(agg_done, groups(i, b, RING))
                    for k, first in enumerate(firsts):
                        sp.dma_start(win[:, b, k].rearrange("p c w -> p (c w)"),
                                     rows[bass.ds(first, WINDOW), :].rearrange(
                                         "(p c) w -> p (c w)", c=2)).then_inc(win_in[b], 16)
                    if group_has(i, b, RING):
                        sp.wait_ge(pre_ready, groups(i, b, RING))
                        sp.wait_ge(ra_ready, groups(i, b, RING))
                        sp.dma_start(xin[:, b], tile_rows(table, i, b)).then_inc(x_in[b], 16)
                if b % 2 == 1 and group_alive(i, b, 8):
                    sp.wait_ge(fin_ready, groups(i, b, 8))
                    sp.dma_start(tile_rows(out, i, b - 9, 2),
                                 fin[:, b - 1:b + 1].rearrange("p g k w -> p (g k) w")
                                 ).then_inc(stored[b // 2], 16)

            node_steps(sp, step)
            for h in range(2):
                sp.wait_ge(stored[h], 16 * ((NG // 2 + 1 - h) // 2))

        @block.gpsimd
        def _(pool):
            nc.gpsimd.memset(ident[:], 0.0).then_inc(consts_set, 1)
            nc.gpsimd.memset(msg[:, :, CNT], 1.0).then_inc(consts_ready, 1)
            nc.gpsimd.memset(ones[:], 1.0).then_inc(consts_ready, 1)
            nc.gpsimd.memset(eps[:], EPS).then_inc(consts_ready, 1)
            pool.wait_ge(consts_set, 1)
            nc.gpsimd.affine_select(out=ident[:], in_=ident[:], compare_op=ALU.not_equal, fill=1.0,
                                    base=0, pattern=[[-1, P]], channel_multiplier=1
                                    ).then_inc(consts_ready, 1)
            pool.wait_ge(srcs_in, 16)

            def more_constants():
                for ap, pattern, base, mult in (
                        (column, [[1, P]], 0, 0), (tile_base, [[P, NT]], 0, 0),
                        (bound, [[P * P, CH]], 0, P), (node_base, [[P, NT]], BASE, 0),
                        (g_label, [[1, ROWS // P]], 0, ROWS // P), (g_spare, [[0, 1]], NP, 1)):
                    nc.gpsimd.iota(ap[:].bitcast(I32), pattern=pattern, base=base,
                                   channel_multiplier=mult).then_inc(iotas_set, 1)
                nc.gpsimd.memset(pads[:], 0.0).then_inc(pads_set, 1)
                nc.gpsimd.memset(later_mask[:], 1.0).then_inc(pads_set, 1)
                pool.wait_ge(pads_set, 2)
                nc.gpsimd.memset(pads[:, :, LABEL], -1.0).then_inc(pads_ready, 1)
                nc.gpsimd.affine_select(out=later_mask[:], in_=later_mask[:],
                                        compare_op=ALU.is_gt, fill=0.0, base=0,
                                        pattern=[[1, P]], channel_multiplier=-1
                                        ).then_inc(mask_ready, 1)

            def step(i, j):
                if not alive(i, j, 0):
                    return
                if j % 2 == 0:
                    for n in range(4):
                        if has(i, j, PAIRS):
                            pool.wait_ge(gathered[2 * j + n], 16 * i)
                    nc.gpsimd.tensor_copy(src_now[:, 2 * j:2 * j + 4],
                                          srcs[:, bass.ds(i * BLOCK + 2 * j, 4)]
                                          ).then_inc(src_ready, 1)
                    pool.wait_ge(src_ready, 2 * i + (j // 2 + 1))
                if has(i, j, PAIRS):
                    pool.wait_ge(t_ready, done(i, j, PAIRS))
                pool.sem_inc(gather_go, 1)
                for n in (2 * j, 2 * j + 1):
                    pool.indirect_dma_start(
                        out=gat[:, n, 0:XW], out_offset=None, in_=table,
                        in_offset=bass.IndirectOffsetOnAxis(ap=src_now[:, n:n + 1], axis=0)
                    ).then_inc(gathered[n], 16)

            def find_windows():
                pool.wait_ge(at_tile_i_ready, 1)
                for c in range(CH):
                    pool.indirect_dma_start(
                        out=picked[:, c, :], out_offset=None,
                        in_=dst_rows.rearrange("(t p) -> t p", p=P),
                        in_offset=bass.IndirectOffsetOnAxis(ap=at_tile_i[:, c:c + 1], axis=0)
                    ).then_inc(picked_in, 16)

            edge_steps(pool, step, {(0, 1): more_constants, (1, 3): find_windows})

            pool.wait_ge(prepared, 1)
            with pool.If(pool.value_load(general_i[0:1, 0:1], min_val=0, max_val=1) != 0):
                with pool.Fori(0, T) as t:
                    pool.wait_ge(g_sum_ready, t + 1)
                    pool.wait_ge(g_row_ready, t + 1)
                    pool.sem_inc(g_scatter_go, 1)
                    pool.indirect_dma_start(
                        out=rows, out_offset=bass.IndirectOffsetOnAxis(ap=g_row[:, 0:1], axis=0),
                        in_=g_sum[:], in_offset=None, compute_op=ALU.add).then_inc(g_added, 16)

            def step(i, b):
                b0, b3 = b % 2, (b - 3) % 2
                if group_alive(i, b, 0):
                    pool.wait_ge(x_in[b], 16 * (i + 1))
                    if group_has(i, b, 2):
                        pool.wait_ge(xt_ready, groups(i, b, 2))
                    for xa, n, w in ((xa0, 1, MUL0), (xa1, 1 + MUL0, VEC)):
                        last = nc.gpsimd.tensor_tensor(
                            xa[:, b0], xin[:, b, :, n:n + w],
                            xin[:, b, :, 0:1].broadcast_to([P, GROUP, w]), ALU.mult)
                    last.then_inc(xa_ready, 1)
                    pool.wait_ge(win_in[b], 16 * GROUP * (i + 1))
                    if group_has(i, b, 2):
                        pool.wait_ge(hot_ready, groups(i, b, 2))
                    nc.gpsimd.tensor_tensor(
                        lab[:, b0], win[:, b, :, :, LABEL],
                        tile_base[0:WP, bass.ds((RING * i + b) * GROUP, GROUP)].unsqueeze(2)
                        .broadcast_to([WP, GROUP, 2]), ALU.subtract).then_inc(lab_ready, 1)
                if group_alive(i, b, 3):
                    slot = (b - 3) % RING
                    pool.wait_ge(agg_ready, groups(i, b, 3))
                    pool.wait_ge(pre_ready, groups(i, b, 3))
                    if group_has(i, b, 3 + RING):
                        pool.wait_ge(fin_ready, groups(i, b, 3 + RING))
                    nc.gpsimd.tensor_tensor(res[:, slot], agg[:, b3], pre[:, b3], ALU.add
                                            ).then_inc(res_ready, 1)

            node_steps(pool, step)

        @block.tensor
        def _(pe):
            pe.wait_ge(weights_in, 32)
            pe.wait_ge(consts_ready, 4)
            pe.wait_ge(wy_ready, 5)

            def step(i, j):
                b0, b1, b2 = j % 2, (j - 1) % 2, (j - 2) % 2
                if alive(i, j, 0):
                    if has(i, j, 1):
                        pe.wait_ge(t_out, done(i, j, 1))
                    pe.wait_ge(q_ready, done(i, j))
                    nc.tensor.transpose(t_ps[:, 0, :],
                                        x0[:, b0].rearrange("p s w -> p (s w)"), ident[:])
                    for s in range(2):
                        last = nc.tensor.transpose(t_ps[:, 1 + s, :],
                                                   gat[:, 2 * j + s, 1 + MUL0:GW], ident[:])
                    last.then_inc(t_ready, 1)
                    if has(i, j, 1):
                        pe.wait_ge(h_out, done(i, j, 1))
                    nc.tensor.matmul(h_ps, wt[:, W_H + j * P:W_H + (j + 1) * P],
                                     eas[:, i, :] if isinstance(i, int)
                                     else eas[:, bass.ds(i, 1), :].squeeze(1),
                                     start=True, stop=True).then_inc(h_ready, 1)
                if alive(i, j, 1):
                    pe.wait_ge(t_out, done(i, j, 1))
                    if has(i, j, 2):
                        pe.wait_ge(e_out, done(i, j, 2))
                    nc.tensor.matmul(e_ps[:, 0, :], wt[:, W_E0:W_E0 + P], t_sb[:, b1, 0, :],
                                     start=True, stop=True)
                    nc.tensor.matmul(e_ps[:, 1:3, :].rearrange("p s e -> p (s e)"),
                                     wt[:, W_E1:W_E1 + P],
                                     t_sb[:, b1, 1:3, :].rearrange("p s e -> p (s e)"),
                                     start=True, stop=True).then_inc(e_ready, 1)
                    pe.wait_ge(h_out, done(i, j, 1))
                    if has(i, j, 2):
                        pe.wait_ge(mid_ready, done(i, j, 2))
                    for c in range(4):
                        w = W_W + c * P
                        last = nc.tensor.matmul(w_ps[:, c, :], wt[:, w:w + P], h_sb[:, b1, :],
                                                start=True, stop=True)
                    last.then_inc(w_ready, 1)
                if alive(i, j, 2):
                    pe.wait_ge(mid_ready, done(i, j, 2))
                    if has(i, j, 3):
                        pe.wait_ge(msg_ready, done(i, j, 3))
                    nc.tensor.matmul(y_ps[:, :, 0:1 + MUL0], mid[:, b2, 0, :],
                                     wy[:, 0:W_YB - W_Y0], start=True, stop=True)
                    nc.tensor.matmul(yb_ps.rearrange("p s w -> p (s w)"), mid[:, b2, 1, :],
                                     wy[:, W_YB - W_Y0:W_Y1 - W_Y0], start=True, stop=True)
                    for s in range(2):
                        last = nc.tensor.matmul(y_ps[:, s, 1 + MUL0:YW], mid[:, b2, 2 + s, :],
                                                wy[:, W_Y1 - W_Y0:W_S0 - W_Y0],
                                                start=True, stop=True)
                    last.then_inc(y_ready, 1)
            def spread_heads():
                pe.wait_ge(heads_ready, 1)
                nc.tensor.matmul(heads_ps, ones[0:1, :], heads[:], start=True,
                                 stop=True).then_inc(heads_spread, 1)
                pe.wait_ge(wrong_ready, 1)
                nc.tensor.matmul(wrong_ps, wrong[:], ones[:, 0:1], start=True,
                                 stop=True).then_inc(wrong_summed, 1)

            def wait_rest():
                pe.wait_ge(rest_in, 16 + 16 * REST)

            edge_steps(pe, step, {(0, 2): spread_heads, (1, 3): wait_rest})

            pe.wait_ge(prepared, 1)
            with pe.If(pe.value_load(general_i[0:1, 0:1], min_val=0, max_val=1) != 0):
                with pe.Fori(0, T) as t:
                    pe.wait_ge(g_same_ready, t + 1)
                    nc.tensor.matmul(g_ps, g_same[:], g_msg[:, 0:SW], start=True,
                                     stop=True).then_inc(g_summed, 1)

            def step(i, b):
                if group_alive(i, b, 0):
                    if group_has(i, b, 1):
                        pe.wait_ge(xt_out, groups(i, b, 1))
                    pe.wait_ge(xa_ready, groups(i, b))
                    for k in range(GROUP // 2):
                        nc.tensor.transpose(xt0_ps[:, k, :],
                                            xa0[:, b % 2, 2 * k:2 * k + 2, :].rearrange(
                                                "p k w -> p (k w)"), ident[:])
                    for k in range(GROUP):
                        last = nc.tensor.transpose(xt1_ps[:, k, :], xa1[:, b % 2, k, :],
                                                   ident[:])
                    last.then_inc(xt_ready, 1)
                if group_alive(i, b, 1):
                    b1 = (b - 1) % 2
                    pe.wait_ge(hot_ready, groups(i, b, 1))
                    if group_has(i, b, 3):
                        pe.wait_ge(agg_ready, groups(i, b, 3))
                    for k in range(GROUP):
                        for c in range(2):
                            last = nc.tensor.matmul(agg_ps[b1][:, k, 0:SW], hot[:, b1, k, c, :],
                                                    win[:, (b - 1) % RING, k, c, 0:SW],
                                                    start=c == 0, stop=c == 1)
                    last.then_inc(agg_done, 1)
                    pe.wait_ge(xt_out, groups(i, b, 1))
                    if group_has(i, b, 2):
                        pe.wait_ge(pre_ready, groups(i, b, 2))
                    for k in range(GROUP // 2):
                        nc.tensor.matmul(sc0_ps[:, k, :], xt0[:, b1, k, :],
                                         wy[:, W_S0 - W_Y0:W_S1 - W_Y0], start=True, stop=True)
                    for k in range(GROUP):
                        last = nc.tensor.matmul(
                            sc1_ps[:, k // 2, k % 2 * VEC:k % 2 * VEC + VEC], xt1[:, b1, k, :],
                            wy[0:VEC, W_S1 - W_Y0:WC - W_Y0], start=True, stop=True)
                    last.then_inc(sc_ready, 1)

            pe.wait_ge(msg_ready, NQ)
            node_steps(pe, step)

        @block.scalar
        def _(act):
            act.wait_ge(consts_ready, 4)
            nc.scalar.activation(std[:, 0, 0:1], eps[:], ACT.Silu).then_inc(table_ready, 1)

            def step(i, j):
                b0, b1, b2 = j % 2, (j - 1) % 2, (j - 2) % 2
                if alive(i, j, 0):
                    act.wait_ge(t_ready, done(i, j))
                    if has(i, j, 2):
                        act.wait_ge(e_ready, done(i, j, 2))
                    nc.scalar.activation(t_sb[:, b0].rearrange("p c e -> p (c e)"),
                                         t_ps.rearrange("p c e -> p (c e)"),
                                         ACT.Copy).then_inc(t_out, 1)
                    act.wait_ge(h_ready, done(i, j))
                    if has(i, j, 2):
                        act.wait_ge(w_ready, done(i, j, 2))
                    nc.scalar.activation(h_sb[:, b0, :], h_ps, ACT.Silu,
                                         scale=FC_IN ** -0.5).then_inc(h_out, 1)
                if alive(i, j, 1):
                    act.wait_ge(e_ready, done(i, j, 1))
                    if has(i, j, 3):
                        act.wait_ge(mid_ready, done(i, j, 3))
                    nc.scalar.activation(e_sb[:, b1].rearrange("p c e -> p (c e)"),
                                         e_ps.rearrange("p c e -> p (c e)"),
                                         ACT.Copy).then_inc(e_out, 1)
                if alive(i, j, 2):
                    act.wait_ge(y_ready, done(i, j, 2))
                    if has(i, j, 4):
                        act.wait_ge(msg_ready, done(i, j, 4))
                    nc.scalar.activation(z[:, b2, :, 0:1 + MUL0], y_ps[:, :, Y_C:YW],
                                         ACT.Copy).then_inc(zc_ready, 1)
            edge_steps(act, step)

            def step(i, b):
                b0, b1 = b % 2, (b - 1) % 2
                if group_alive(i, b, 5):
                    past = (b - 5) % RING
                    act.wait_ge(mv_ready, groups(i, b, 5))
                    if group_has(i, b, 5 + RING):
                        act.wait_ge(rstd_ready, groups(i, b, 5 + RING))
                    else:
                        act.wait_ge(table_ready, 1)
                    nc.scalar.activation(std[:, past], mv[:, past, :, 1], ACT.Sqrt,
                                         bias=eps[:, 0:1]).then_inc(std_ready, 1)
                if group_alive(i, b, 0):
                    act.wait_ge(xt_ready, groups(i, b))
                    if group_has(i, b, 2):
                        act.wait_ge(sc_ready, groups(i, b, 2))
                    nc.scalar.activation(xt0[:, b0].rearrange("p k e -> p (k e)"),
                                         xt0_ps.rearrange("p k e -> p (k e)"), ACT.Copy)
                    nc.scalar.activation(xt1[:, b0].rearrange("p k e -> p (k e)"),
                                         xt1_ps.rearrange("p k e -> p (k e)"),
                                         ACT.Copy).then_inc(xt_out, 1)
                if group_alive(i, b, 2):
                    act.wait_ge(coef_ready, groups(i, b, 2))
                    if group_has(i, b, 4):
                        act.wait_ge(res_ready, groups(i, b, 4))
                    for k in range(GROUP):
                        last = nc.scalar.activation(agg[:, b0, k, :], agg_ps[b0][:, k, 1:1 + D],
                                                    ACT.Copy, scale=coef[:, b0, k:k + 1])
                    last.then_inc(agg_ready, 1)
                if group_alive(i, b, 5):
                    act.wait_ge(shift_ready, groups(i, b, 5))
                    if past % 2 == 0 and group_has(i, b, 5 + RING):
                        act.wait_ge(stored[past // 2], 16 * (i + (b - 5 - past) // RING))
                    for k in range(GROUP):
                        last = nc.scalar.activation(fin[:, past, k, :], res[:, past, k, :],
                                                    ACT.Identity, bias=shift[:, past, k:k + 1],
                                                    scale=rstd[:, past, k:k + 1])
                    last.then_inc(fin_ready, 1)

            node_steps(act, step)

        @block.vector
        def _(dve):
            dve.wait_ge(weights_in, 32)
            nc.vector.tensor_scalar(wy[:, 0:W_Y1 - W_Y0], wt[:, W_Y0:W_Y1], inv_fc * inv8 * inv96,
                                    None, ALU.mult).then_inc(wy_ready, 1)
            nc.vector.tensor_scalar(wy[0:VEC, W_Y1 - W_Y0:W_S0 - W_Y0], wt[0:VEC, W_Y1:W_S0],
                                    inv_fc * inv32 * inv96, None, ALU.mult).then_inc(wy_ready, 1)
            nc.vector.tensor_scalar(wy[VEC:P, W_Y1 - W_Y0:W_S0 - W_Y0], wt[VEC:P, W_Y1:W_S0],
                                    inv_fc * inv32 * inv96 * 3 ** -0.5, None,
                                    ALU.mult).then_inc(wy_ready, 1)
            nc.vector.tensor_scalar(wy[:, W_S0 - W_Y0:W_S1 - W_Y0], wt[:, W_S0:W_S1], inv8,
                                    None, ALU.mult).then_inc(wy_ready, 1)
            nc.vector.tensor_scalar(wy[:, W_S1 - W_Y0:WC - W_Y0], wt[:, W_S1:WC], inv32,
                                    None, ALU.mult).then_inc(wy_ready, 1)
            dve.wait_ge(tables_in, 32)
            nc.vector.tensor_copy(dsts[:], dsts_i[:]).then_inc(dsts_ready, 1)
            dve.wait_ge(consts_ready, 4)
            dve.wait_ge(dsts_ready, 1)

            def at(i, j):
                return bass.ds(i * BLOCK + 2 * j, 2)

            def step(i, j):
                b0, b1 = j % 2, (j - 1) % 2
                i3 = i if j == 3 else i - 1
                j3 = (j - 3) % PAIRS
                n = 2 * j
                if alive(i, j, 0):
                    if has(i, j, PAIRS):
                        dve.wait_ge(msg_ready, done(i, j, PAIRS))
                    for s in range(2):
                        dve.wait_ge(gathered[n + s], 16 * (i + 1))
                    nc.vector.tensor_tensor(sha[:, j], shs[:, at(i, j), :],
                                            gat[:, n:n + 2, 0:1].broadcast_to([P, 2, 4]),
                                            ALU.mult).then_inc(sha_ready, 1)
                if alive(i, j, 0):
                    if has(i, j, 1):
                        dve.wait_ge(q_ready, done(i, j, 1))
                    dve.wait_ge(sha_ready, done(i, j))
                    nc.vector.tensor_tensor(
                        qprod[:],
                        gat[:, n:n + 2, 1 + MUL0:XW].rearrange("p s (u m) -> p s u m", m=3),
                        sha[:, j, :, 1:4].unsqueeze(2).broadcast_to([P, 2, MUL1, 3]),
                        ALU.mult).then_inc(qprod_ready, 1)
                if alive(i, j, 0):
                    if has(i, j, 2):
                        dve.wait_ge(t_ready, done(i, j, 2))
                    nc.vector.tensor_copy(x0[:, b0], gat[:, n:n + 2, 1:1 + MUL0])
                    dve.wait_ge(qprod_ready, done(i, j))
                    nc.vector.tensor_reduce(gat[:, n:n + 2, QX:GW], qprod[:], AX_X,
                                            ALU.add).then_inc(q_ready, 1)
                if alive(i, j, 2):
                    dve.wait_ge(w_ready, done(i, j, 2))
                    dve.wait_ge(e_out, done(i, j, 2))
                    if has(i, j, 4):
                        dve.wait_ge(y_ready, done(i, j, 4))
                    nc.vector.tensor_tensor(mid[:, b0, 0:2, :], w_ps[:, 0:2, :],
                                            e_sb[:, b0, 0:1, :].broadcast_to([P, 2, P]),
                                            ALU.mult)
                    nc.vector.tensor_tensor(mid[:, b0, 2:4, :], w_ps[:, 2:4, :],
                                            e_sb[:, b0, 1:3, :], ALU.mult
                                            ).then_inc(mid_ready, 1)
                if alive(i, j, 3):
                    dve.wait_ge(y_ready, done(i, j, 3))
                    if has(i, j, 5):
                        dve.wait_ge(msg_ready, done(i, j, 5))
                    nc.vector.tensor_tensor(
                        z[:, b1, :, 1 + MUL0:].rearrange("p s (v m) -> p s v m", m=3),
                        yb_ps.unsqueeze(3).broadcast_to([P, 2, MUL1, 3]),
                        sha[:, j3, :, 1:4].unsqueeze(2).broadcast_to([P, 2, MUL1, 3]),
                        ALU.mult).then_inc(zb_ready, 1)
                if alive(i, j, 3):
                    if has(i, j, 3 + PAIRS):
                        dve.wait_ge(messages_out[j3 // 2], 16 * (i3 + 0))
                    nc.vector.tensor_copy(msg[:, 2 * j3:2 * j3 + 2, LABEL], dsts[:, at(i3, j3)]
                                          ).then_inc(label_ready, 1)
                if alive(i, j, 3):
                    dve.wait_ge(zb_ready, done(i, j, 3))
                    dve.wait_ge(zc_ready, done(i, j, 3))
                    for s in range(2):
                        last = nc.vector.scalar_tensor_tensor(
                            out=msg[:, 2 * j3 + s, 0:1 + D], in0=y_ps[:, s, 0:Y_C],
                            scalar=sha[:, j3, s, 0:1], in1=z[:, b1, s, :],
                            op0=ALU.mult, op1=ALU.add)
                    last.then_inc(msg_ready, 1)

            def prepare_order():
                dve.wait_ge(order_in, 48)
                nc.vector.tensor_copy(heads[:], heads_i[:]).then_inc(heads_ready, 1)
                nc.vector.tensor_tensor(greater[:], seq[:, 0, :], seq[:, 1, :],
                                        ALU.is_gt).then_inc(greater_ready, 1)
                dve.wait_ge(iotas_set, 6)
                for ap in (column, tile_base, bound, node_base, g_label, g_spare):
                    nc.vector.tensor_copy(ap[:], ap[:].bitcast(I32)).then_inc(iotas_ready, 1)
                dve.wait_ge(greater_ready, 1)
                nc.vector.tensor_reduce(wrong[:], greater[:], AX_X, ALU.add
                                        ).then_inc(wrong_ready, 1)

            def prepare_tiles():
                dve.wait_ge(heads_spread, 1)
                dve.wait_ge(iotas_ready, 6)
                for c in range(CH):
                    last = nc.vector.tensor_scalar(below[:, c, :], heads_ps, bound[:, c:c + 1],
                                                   None, ALU.is_lt)
                last.then_inc(below_ready, 1)
                dve.wait_ge(below_ready, 1)
                nc.vector.tensor_reduce(tiles_below[:], below[:], AX_X, ALU.add
                                        ).then_inc(tiles_below_ready, 1)
                dve.wait_ge(tiles_below_ready, 1)
                nc.vector.tensor_scalar(at_tile[:], tiles_below[:], -1.0, 0.0, ALU.add, ALU.max
                                        ).then_inc(at_tile_ready, 1)
                dve.wait_ge(at_tile_ready, 1)
                nc.vector.tensor_copy(at_tile_i[:], at_tile[:]).then_inc(at_tile_i_ready, 1)

            def clear():
                nc.vector.memset(zeros[:], 0.0).then_inc(zeros_set, 1)
                nc.vector.memset(g_sum[:], 0.0).then_inc(zeros_set, 1)

            def prepare_starts():
                dve.wait_ge(rest_in, 16 + 16 * REST)
                dve.wait_ge(picked_in, 16 * CH)
                nc.vector.tensor_tensor(picked_below[:], picked[:],
                                        bound[:].unsqueeze(2).broadcast_to([P, CH, P]),
                                        ALU.is_lt).then_inc(picked_below_ready, 1)
                dve.wait_ge(picked_below_ready, 1)
                nc.vector.tensor_reduce(in_tile[:], picked_below[:], AX_X, ALU.add
                                        ).then_inc(in_tile_ready, 1)
                dve.wait_ge(in_tile_ready, 1)
                nc.vector.scalar_tensor_tensor(out=starts[:], in0=at_tile[:], scalar=float(P),
                                               in1=in_tile[:], op0=ALU.mult, op1=ALU.add
                                               ).then_inc(starts_ready, 1)

            def prepare_flag():
                dve.wait_ge(starts_in, 16)
                nc.vector.tensor_tensor(widths[:], start_row[:, 1:NT + 1], start_row[:, 0:NT],
                                        ALU.subtract).then_inc(widths_ready, 1)
                dve.wait_ge(widths_ready, 1)
                nc.vector.tensor_reduce(widest[:], widths[:], AX_X, ALU.max
                                        ).then_inc(widest_ready, 1)
                dve.wait_ge(widest_ready, 1)
                dve.wait_ge(wrong_summed, 1)
                nc.vector.scalar_tensor_tensor(out=general[:], in0=widest[:],
                                               scalar=float(WINDOW), in1=wrong_ps,
                                               op0=ALU.is_gt, op1=ALU.add
                                               ).then_inc(over_ready, 1)
                dve.wait_ge(over_ready, 1)
                nc.vector.tensor_scalar(general[:], general[:], 1.0, None, ALU.min
                                        ).then_inc(general_ready, 1)
                nc.vector.tensor_tensor(moved_start[:], node_base[:], start_row[:, 0:NT],
                                        ALU.subtract).then_inc(moved_start_ready, 1)
                dve.wait_ge(general_ready, 1)
                nc.vector.tensor_copy(general_i[:], general[:])
                dve.wait_ge(moved_start_ready, 1)
                nc.vector.scalar_tensor_tensor(out=start_i[:], in0=moved_start[:],
                                               scalar=general[:, 0:1],
                                               in1=start_row[:, 0:NT], op0=ALU.mult, op1=ALU.add
                                               ).then_inc(prepared, 1)

            edge_steps(dve, step, {(0, 1): prepare_order, (0, 3): prepare_tiles, (1, 0): clear,
                                   (1, 3): prepare_starts, NB: prepare_flag})

            dve.wait_ge(prepared, 1)
            with dve.If(dve.value_load(general_i[0:1, 0:1], min_val=0, max_val=1) != 0):
                dve.wait_ge(mask_ready, 1)
                dve.wait_ge(zeros_set, 2)
                with dve.Fori(0, T) as t:
                    dve.wait_ge(g_loaded, 32 * t + 32)
                    nc.vector.tensor_scalar(g_same[:], g_dst[:], g_msg[:, LABEL:AW], None,
                                            ALU.is_equal).then_inc(g_same_ready, 1)
                    nc.vector.tensor_tensor(g_moved[:], g_spare[:], g_msg[:, LABEL:AW],
                                            ALU.subtract).then_inc(g_spare_ready, 1)
                    dve.wait_ge(g_same_ready, t + 1)
                    nc.vector.tensor_tensor(g_junk[:], g_same[:], later_mask[:], ALU.mult
                                            ).then_inc(g_later_ready, 1)
                    dve.wait_ge(g_later_ready, t + 1)
                    nc.vector.tensor_reduce(g_later[:], g_junk[:], AX_X, ALU.max
                                            ).then_inc(g_moved_ready, 1)
                    dve.wait_ge(g_moved_ready, t + 1)
                    dve.wait_ge(g_spare_ready, t + 1)
                    nc.vector.tensor_scalar(g_moved[:], g_moved[:], g_later[:, 0:1],
                                            float(BASE), ALU.mult, ALU.add
                                            ).then_inc(g_offset_ready, 1)
                    dve.wait_ge(g_offset_ready, t + 1)
                    nc.vector.tensor_tensor(g_row[:], g_moved[:], g_msg[:, LABEL:AW], ALU.add
                                            ).then_inc(g_row_ready, 1)
                    dve.wait_ge(g_summed, t + 1)
                    nc.vector.tensor_copy(g_sum[:, 0:SW], g_ps).then_inc(g_sum_ready, 1)

            def step(i, b):
                b0, past = b % 2, (b - 5) % RING
                if group_alive(i, b, 2):
                    slot = (b - 2) % RING
                    g = groups(i, b, 2)
                    dve.wait_ge(agg_done, g)
                    nc.vector.tensor_scalar(cnt[:, b0], agg_ps[b0][:, :, CNT], 1.0, None,
                                            ALU.max).then_inc(cnt_ready, 1)
                    dve.wait_ge(sc_ready, g)
                    if group_has(i, b, 4):
                        dve.wait_ge(res_ready, groups(i, b, 4))
                    for sc, n, w in ((sc0_ps, 0, MUL0), (sc1_ps, MUL0, VEC)):
                        last = nc.vector.tensor_tensor(
                            pre[:, b0, :, n:n + w].rearrange("p (c k) w -> p c k w", k=2),
                            sc.rearrange("p c (k w) -> p c k w", k=2),
                            xin[:, slot, :, 1 + n:1 + n + w].rearrange(
                                "p (c k) w -> p c k w", k=2), ALU.add)
                    last.then_inc(pre_ready, 1)
                    dve.wait_ge(cnt_ready, g)
                    nc.vector.reciprocal(rcnt[:, b0], cnt[:, b0]).then_inc(rcnt_ready, 1)
                if group_alive(i, b, 4):
                    dve.wait_ge(res_ready, groups(i, b, 4))
                    if group_has(i, b, 4 + RING):
                        dve.wait_ge(mv_ready, groups(i, b, 4 + RING))
                    nc.vector.bn_stats(stats[:, b, 0, :], res[:, b, 0, :])
                if group_alive(i, b, 2):
                    dve.wait_ge(rcnt_ready, g)
                    nc.vector.tensor_tensor(ra[:, b0], rcnt[:, b0], xin[:, slot, :, 0],
                                            ALU.mult).then_inc(ra_ready, 1)
                if group_alive(i, b, 4):
                    nc.vector.bn_stats(stats[:, b, 1, :], res[:, b, 1, :])
                if group_alive(i, b, 2):
                    dve.wait_ge(ra_ready, g)
                    nc.vector.tensor_tensor(rr[:, b0], ra[:, b0], ra[:, b0],
                                            ALU.mult).then_inc(rr_ready, 1)
                if group_alive(i, b, 4):
                    nc.vector.bn_stats(stats[:, b, 2, :], res[:, b, 2, :])
                if group_alive(i, b, 2):
                    dve.wait_ge(rr_ready, g)
                    nc.vector.tensor_tensor(coef[:, b0], rr[:, b0], agg_ps[b0][:, :, GATE],
                                            ALU.mult).then_inc(coef_ready, 1)
                if group_alive(i, b, 4):
                    nc.vector.bn_stats(stats[:, b, 3, :], res[:, b, 3, :]
                                       ).then_inc(stats_ready, 1)
                if group_alive(i, b, 0):
                    dve.wait_ge(lab_ready, groups(i, b))
                    if group_has(i, b, 2):
                        dve.wait_ge(agg_done, groups(i, b, 2))
                    nc.vector.tensor_tensor(
                        hot[:, b0].rearrange("p k c e -> p (k c) e"),
                        column[0:WP, :].unsqueeze(1).broadcast_to([WP, 2 * GROUP, P]),
                        lab[:, b0].rearrange("p k c -> p (k c)").unsqueeze(2)
                        .broadcast_to([WP, 2 * GROUP, P]), ALU.is_equal).then_inc(hot_ready, 1)
                if group_alive(i, b, 5):
                    dve.wait_ge(std_ready, groups(i, b, 5))
                    if group_has(i, b, 5 + RING):
                        dve.wait_ge(fin_ready, groups(i, b, 5 + RING))
                    nc.vector.reciprocal(rstd[:, past], std[:, past]).then_inc(rstd_ready, 1)
                if group_alive(i, b, 4):
                    dve.wait_ge(stats_ready, groups(i, b, 4))
                    dve.sem_inc(aggr_go, 1)
                    for k in range(GROUP):
                        last = nc.vector.bn_aggr(mv[:, b, k, :], stats[:, b, k, :])
                    last.then_inc(mv_ready, 1)
                if group_alive(i, b, 5):
                    dve.wait_ge(rstd_ready, groups(i, b, 5))
                    nc.vector.scalar_tensor_tensor(
                        out=shift[:, past], in0=mv[:, past, :, 0], scalar=-1.0,
                        in1=rstd[:, past], op0=ALU.mult, op1=ALU.mult
                    ).then_inc(shift_ready, 1)

            node_steps(dve, step)


def pack_weights(np, Wfc1, Wfc2, Wsc0, Wsc1, Wl1_0, Wl1_1, Wl2_s, Wl2_v, Wa):
    w = np.zeros((P, WC), np.float32)
    for pair in range(PAIRS):
        for s in range(2):
            row = (2 * pair + s) * FC_IN
            col = W_H + pair * P + s * FC_H
            w[row:row + FC_IN, col:col + FC_H] = Wfc1
    for s in range(2):
        half = slice(s * MUL0, (s + 1) * MUL0)
        rows = slice(s * FC_H, (s + 1) * FC_H)
        for c in range(2):
            col = W_W + c * P + s * MUL0
            w[rows, col:col + MUL0] = Wfc2[:, c * MUL0:(c + 1) * MUL0]
        col = W_W + (2 + s) * P
        for m in range(3):
            w[rows, col + m:col + VEC:3] = Wfc2[:, P:P + MUL1]
        w[rows, col + VEC:col + P] = Wfc2[:, P + MUL1:]
        w[half, W_E0 + s * MUL0:W_E0 + (s + 1) * MUL0] = Wl1_0
        w[half, W_S0 + s * MUL0:W_S0 + (s + 1) * MUL0] = Wsc0
        w[half, W_Y0 + s * (1 + MUL0)] = Wa[:MUL0, 0]
        w[half, W_Y0 + s * (1 + MUL0) + 1:W_Y0 + (s + 1) * (1 + MUL0)] = Wl2_s[:MUL0]
        w[half, W_YB + s * MUL1:W_YB + (s + 1) * MUL1] = Wl2_v[:MUL0]
    for m in range(3):
        w[m:VEC:3, W_E1 + m:W_E1 + VEC:3] = Wl1_1
        w[m:VEC:3, W_Y1 + m:W_Y1 + VEC:3] = Wl2_v[MUL0:]
        w[m:VEC:3, W_S1 + m:W_S1 + VEC:3] = Wsc1
    w[VEC:P, W_E1 + VEC:W_E1 + P] = Wl1_1
    w[VEC:P, W_Y1 + VEC] = Wa[MUL0:, 0]
    w[VEC:P, W_Y1 + VEC + 1:W_S0] = Wl2_s[MUL0:]
    return w


def kernel(x, src, dst, edge_attr_16, edge_attr_4, node_vec1, **weights):
    import numpy as np
    import concourse.bacc as bacc
    from concourse.bass_utils import run_bass_kernel_spmd

    x, src, dst, ea, sh, a = (np.asarray(v) for v in
                              (x, src, dst, edge_attr_16, edge_attr_4, node_vec1))
    named = {k.removeprefix("L0_gnn_"): np.asarray(v) for k, v in weights.items()}
    N, E = x.shape[0], src.shape[0]
    NP = (N // (2 * GROUP * P) + 1) * 2 * GROUP * P
    T = -(-E // (BLOCK * P)) * BLOCK
    EP = T * P

    def rows(v, n, fill=0):
        return np.concatenate([v, np.full((n - v.shape[0],) + v.shape[1:], fill, v.dtype)])

    def tiles(v):
        v = v.reshape(T // 4, P, 4, -1).transpose(1, 0, 2, 3)
        return np.ascontiguousarray(v).reshape(P, -1)

    dst_p = rows(dst, EP, NP - 1)
    arrays = {
        "table": rows(np.concatenate([a, x], 1), NP),
        "src_t": tiles(rows(src, EP)),
        "dst_t": tiles(dst_p),
        "dst_rows": rows(dst, EP + P, NP - 1),
        "sh_t": tiles(rows(sh, EP)),
        "ea_t": np.ascontiguousarray(
            rows(ea, EP).reshape(T // BLOCK, 2, P, 4, FC_IN).transpose(1, 3, 4, 0, 2)
        ).reshape(P, T // BLOCK * P),
        "weights": pack_weights(np, **named),
    }
    nc = bacc.Bacc("TRN2", target_bir_lowering=False, num_devices=1)
    args = [nc.dram_tensor(name, v.shape, mybir.dt.from_np(v.dtype), kind="ExternalInput").ap()
            for name, v in arrays.items()]
    out = nc.dram_tensor("out", (NP, D), F32, kind="ExternalOutput").ap()
    gnn_kernel(nc, *args, out)
    r = run_bass_kernel_spmd(nc, [arrays], core_ids=[0])
    return r.results[0]["out"][:N]
```
